# Optimizing a Trainium2 kernel written in Bass

```python
import numpy as np
import jax
import jax.numpy as jnp

def _softmax(x, axis=-1):
    return jax.nn.softmax(x, axis=axis)

def _gelu(x):
    return jax.nn.gelu(x, approximate=True)

def _silu(x):
    return jax.nn.silu(x)

def _sigmoid(x):
    return jax.nn.sigmoid(x)

def _layernorm(x, axis=-1, eps=1e-05):
    m = jnp.mean(x, axis=axis, keepdims=True)
    v = jnp.var(x, axis=axis, keepdims=True)
    return (x - m) / jnp.sqrt(v + eps)

def _scatter_add(tgt, idx, src, axis=0):
    return tgt.at[idx].add(src)

def _segment_sum(src, seg, n):
    return jax.ops.segment_sum(src, seg, n)
kernel_name = 'mk_early_fusion_d1_tok_img512_r4_b153d5'

def setup_inputs(seed: int=0):
    np.random.seed(seed)
    _w = jnp.asarray

    def _rec_inputs():
        import jax
        import jax.numpy as jnp
        _rk = jax.random.key(seed)
        x = -0.000147625 + 0.999875 * jax.random.normal(jax.random.fold_in(_rk, 1), (64, 3, 224, 224), jnp.float32)
        txt = 0.00355565 + 0.408319 * jax.random.normal(jax.random.fold_in(_rk, 2), (64, 128, 128), jnp.float32)
        return (x, txt)
    x, txt = _rec_inputs()

    def _L0_tok_setup():
        import jax, jax.numpy as jnp
        import numpy as np
        N_PATCHES = 8
        PATCH = 28
        C = 3
        IN_D = C * PATCH * PATCH
        HID = 128
        SEQ = N_PATCHES * N_PATCHES + 1

        def _positional_embedding(seq_len, dim):
            i = np.arange(seq_len)[:, None].astype(np.float32)
            j = np.arange(dim)[None, :].astype(np.float32)
            ang = i / np.power(100000.0, j / dim)
            pe = np.where(j % 2 == 0, np.sin(ang), np.cos(ang))
            return jnp.asarray(pe, dtype=jnp.float32)
        key = jax.random.key(seed)
        k1, k2, k3, k4 = jax.random.split(key, 4)
        B = 64
        X = jax.random.normal(k1, (B, C, 224, 224), dtype=jnp.float32)
        bound = 1.0 / np.sqrt(IN_D)
        W = jax.random.uniform(k2, (HID, IN_D), minval=-bound, maxval=bound, dtype=jnp.float32)
        b = jax.random.uniform(k3, (HID,), minval=-bound, maxval=bound, dtype=jnp.float32)
        class_token = jax.random.uniform(k4, (1, HID), dtype=jnp.float32)
        pos_embed = _positional_embedding(SEQ, HID)
        return {'X': X, 'W': W, 'b': b, 'class_token': class_token, 'pos_embed': pos_embed}
    _L0_tok_all = _L0_tok_setup()
    _L0_tok_in = {k: v for k, v in _L0_tok_all.items() if k in ('W', 'b', 'class_token', 'pos_embed')}
    del _L0_tok_all

    def _L0_attn_setup():
        import jax, jax.numpy as jnp
        import numpy as np
        D_MODEL = 128
        N_STATE = 16
        N_HEADS = 8
        D_INNER = 2 * D_MODEL
        D_CONV = 4
        DT_RANK = D_MODEL // 16
        B = 4
        L = 256
        HEAD_DIM = D_MODEL // N_HEADS

        def _ln(x, g, b):
            m = x.mean(-1, keepdims=True)
            v = ((x - m) ** 2).mean(-1, keepdims=True)
            return (x - m) / jnp.sqrt(v + 1e-05) * g + b

        def _mamba(x, in_proj_w, conv_w, conv_b, x_proj_w, dt_proj_w, dt_proj_b, A_log, Dp, out_proj_w):
            b = x.shape[0]
            xz = x @ in_proj_w.T
            u, z = jnp.split(xz, 2, axis=-1)
            uc = jax.lax.conv_general_dilated(u.transpose(0, 2, 1), conv_w, (1,), [(D_CONV - 1, 0)], dimension_numbers=('NCH', 'OIH', 'NCH'), feature_group_count=D_INNER)
            u = jax.nn.silu((uc + conv_b[None, :, None]).transpose(0, 2, 1))
            x_dbl = u @ x_proj_w.T
            dt = jax.nn.softplus(x_dbl[..., :DT_RANK] @ dt_proj_w.T + dt_proj_b)
            Bs = x_dbl[..., DT_RANK:DT_RANK + N_STATE]
            Cs = x_dbl[..., DT_RANK + N_STATE:]
            A = -jnp.exp(A_log)

            def step(h, t):
                dt_t, B_t, C_t, u_t = t
                h = jnp.exp(dt_t[:, :, None] * A) * h + (dt_t * u_t)[:, :, None] * B_t[:, None, :]
                return (h, jnp.einsum('bdn,bn->bd', h, C_t))
            h0 = jnp.zeros((b, D_INNER, N_STATE), x.dtype)
            _, ys = jax.lax.scan(step, h0, (dt.transpose(1, 0, 2), Bs.transpose(1, 0, 2), Cs.transpose(1, 0, 2), u.transpose(1, 0, 2)))
            y = ys.transpose(1, 0, 2) + u * Dp
            return y * jax.nn.silu(z) @ out_proj_w.T

        def _forward(x, in_proj_w, conv_w, conv_b, x_proj_w, dt_proj_w, dt_proj_b, A_log, Dp, out_proj_w, mha_in_w, mha_in_b, mha_out_w, mha_out_b, ln1_g, ln1_b, ln2_g, ln2_b, ln3_g, ln3_b, w1, b1, w2, b2):
            b, l, d = x.shape
            m = _mamba(x, in_proj_w, conv_w, conv_b, x_proj_w, dt_proj_w, dt_proj_b, A_log, Dp, out_proj_w)
            h1 = _ln(m + x, ln1_g, ln1_b)
            qkv = h1 @ mha_in_w.T + mha_in_b
            q, k, v = [t.reshape(b, l, N_HEADS, HEAD_DIM).transpose(0, 2, 1, 3) for t in jnp.split(qkv, 3, axis=-1)]
            s = jnp.einsum('bhqd,bhkd->bhqk', q, k) * (1.0 / float(np.sqrt(HEAD_DIM)))
            o = jnp.einsum('bhqk,bhkd->bhqd', jax.nn.softmax(s, axis=-1), v)
            attn = o.transpose(0, 2, 1, 3).reshape(b, l, d) @ mha_out_w.T + mha_out_b
            h2 = _ln(attn + h1, ln2_g, ln2_b)
            ff = jax.nn.gelu(h2 @ w1.T + b1, approximate=False) @ w2.T + b2
            return _ln(ff + h2, ln3_g, ln3_b)
        key = jax.random.key(seed)
        ks = jax.random.split(key, 16)
        rn = lambda k, s, sc=0.02: jax.random.normal(k, s, jnp.float32) * sc
        return {'x': jax.random.normal(ks[0], (B, L, D_MODEL), jnp.float32), 'in_proj_w': rn(ks[1], (2 * D_INNER, D_MODEL)), 'conv_w': rn(ks[2], (D_INNER, 1, D_CONV), 0.1), 'conv_b': jnp.zeros((D_INNER,), jnp.float32), 'x_proj_w': rn(ks[3], (DT_RANK + 2 * N_STATE, D_INNER)), 'dt_proj_w': rn(ks[4], (D_INNER, DT_RANK), 0.1), 'dt_proj_b': rn(ks[5], (D_INNER,), 0.1), 'A_log': jnp.log(jnp.broadcast_to(jnp.arange(1, N_STATE + 1, dtype=jnp.float32), (D_INNER, N_STATE))), 'Dp': jnp.ones((D_INNER,), jnp.float32), 'out_proj_w': rn(ks[6], (D_MODEL, D_INNER)), 'mha_in_w': rn(ks[7], (3 * D_MODEL, D_MODEL)), 'mha_in_b': jnp.zeros((3 * D_MODEL,), jnp.float32), 'mha_out_w': rn(ks[8], (D_MODEL, D_MODEL)), 'mha_out_b': jnp.zeros((D_MODEL,), jnp.float32), 'ln1_g': jnp.ones((D_MODEL,), jnp.float32), 'ln1_b': jnp.zeros((D_MODEL,), jnp.float32), 'ln2_g': jnp.ones((D_MODEL,), jnp.float32), 'ln2_b': jnp.zeros((D_MODEL,), jnp.float32), 'ln3_g': jnp.ones((D_MODEL,), jnp.float32), 'ln3_b': jnp.zeros((D_MODEL,), jnp.float32), 'w1': rn(ks[9], (4 * D_MODEL, D_MODEL)), 'b1': jnp.zeros((4 * D_MODEL,), jnp.float32), 'w2': rn(ks[10], (D_MODEL, 4 * D_MODEL)), 'b2': jnp.zeros((D_MODEL,), jnp.float32)}
    _L0_attn_all = _L0_attn_setup()
    _L0_attn_in = {k: v for k, v in _L0_attn_all.items() if k in ('in_proj_w', 'conv_w', 'conv_b', 'x_proj_w', 'dt_proj_w', 'dt_proj_b', 'A_log', 'Dp', 'out_proj_w', 'mha_in_w', 'mha_in_b', 'mha_out_w', 'mha_out_b', 'ln1_g', 'ln1_b', 'ln2_g', 'ln2_b', 'ln3_g', 'ln3_b', 'w1', 'b1', 'w2', 'b2')}
    del _L0_attn_all

    def _L0_ffn_setup():
        import jax, jax.numpy as jnp
        import numpy as np
        B, S, D, E, O = (256, 64, 128, 16, 128)
        key = jax.random.key(seed)
        k_x, k_wg, k_bg, k_we, k_be = jax.random.split(key, 5)
        scale_g = 1.0 / np.sqrt(D)
        scale_e = 1.0 / np.sqrt(D)
        return {'x': jax.random.normal(k_x, (B, S, D), dtype=jnp.float32), 'Wg': jax.random.uniform(k_wg, (D, E), jnp.float32, -scale_g, scale_g), 'bg': jax.random.uniform(k_bg, (E,), jnp.float32, -scale_g, scale_g), 'We': jax.random.uniform(k_we, (E, D, O), jnp.float32, -scale_e, scale_e), 'be': jax.random.uniform(k_be, (E, O), jnp.float32, -scale_e, scale_e)}
    _L0_ffn_all = _L0_ffn_setup()
    _L0_ffn_in = {k: v for k, v in _L0_ffn_all.items() if k in ('Wg', 'bg', 'We', 'be')}
    del _L0_ffn_all
    return {'x': x, 'txt': txt, 'L0_tok_W': _L0_tok_in['W'], 'L0_tok_b': _L0_tok_in['b'], 'L0_tok_class_token': _L0_tok_in['class_token'], 'L0_tok_pos_embed': _L0_tok_in['pos_embed'], 'L0_attn_in_proj_w': _L0_attn_in['in_proj_w'], 'L0_attn_conv_w': _L0_attn_in['conv_w'], 'L0_attn_conv_b': _L0_attn_in['conv_b'], 'L0_attn_x_proj_w': _L0_attn_in['x_proj_w'], 'L0_attn_dt_proj_w': _L0_attn_in['dt_proj_w'], 'L0_attn_dt_proj_b': _L0_attn_in['dt_proj_b'], 'L0_attn_A_log': _L0_attn_in['A_log'], 'L0_attn_Dp': _L0_attn_in['Dp'], 'L0_attn_out_proj_w': _L0_attn_in['out_proj_w'], 'L0_attn_mha_in_w': _L0_attn_in['mha_in_w'], 'L0_attn_mha_in_b': _L0_attn_in['mha_in_b'], 'L0_attn_mha_out_w': _L0_attn_in['mha_out_w'], 'L0_attn_mha_out_b': _L0_attn_in['mha_out_b'], 'L0_attn_ln1_g': _L0_attn_in['ln1_g'], 'L0_attn_ln1_b': _L0_attn_in['ln1_b'], 'L0_attn_ln2_g': _L0_attn_in['ln2_g'], 'L0_attn_ln2_b': _L0_attn_in['ln2_b'], 'L0_attn_ln3_g': _L0_attn_in['ln3_g'], 'L0_attn_ln3_b': _L0_attn_in['ln3_b'], 'L0_attn_w1': _L0_attn_in['w1'], 'L0_attn_b1': _L0_attn_in['b1'], 'L0_attn_w2': _L0_attn_in['w2'], 'L0_attn_b2': _L0_attn_in['b2'], 'L0_ffn_Wg': _L0_ffn_in['Wg'], 'L0_ffn_bg': _L0_ffn_in['bg'], 'L0_ffn_We': _L0_ffn_in['We'], 'L0_ffn_be': _L0_ffn_in['be']}

def reference(x, txt, L0_tok_W, L0_tok_b, L0_tok_class_token, L0_tok_pos_embed, L0_attn_in_proj_w, L0_attn_conv_w, L0_attn_conv_b, L0_attn_x_proj_w, L0_attn_dt_proj_w, L0_attn_dt_proj_b, L0_attn_A_log, L0_attn_Dp, L0_attn_out_proj_w, L0_attn_mha_in_w, L0_attn_mha_in_b, L0_attn_mha_out_w, L0_attn_mha_out_b, L0_attn_ln1_g, L0_attn_ln1_b, L0_attn_ln2_g, L0_attn_ln2_b, L0_attn_ln3_g, L0_attn_ln3_b, L0_attn_w1, L0_attn_b1, L0_attn_w2, L0_attn_b2, L0_ffn_Wg, L0_ffn_bg, L0_ffn_We, L0_ffn_be):
    import jax
    import jax.numpy as jnp

    def _L0_tok_ref(X, W, b, class_token, pos_embed):
        import jax, jax.numpy as jnp
        import numpy as np
        N_PATCHES = 8
        PATCH = 28
        C = 3
        IN_D = C * PATCH * PATCH
        HID = 128
        SEQ = N_PATCHES * N_PATCHES + 1

        def _positional_embedding(seq_len, dim):
            i = np.arange(seq_len)[:, None].astype(np.float32)
            j = np.arange(dim)[None, :].astype(np.float32)
            ang = i / np.power(100000.0, j / dim)
            pe = np.where(j % 2 == 0, np.sin(ang), np.cos(ang))
            return jnp.asarray(pe, dtype=jnp.float32)
        B = X.shape[0]
        patches = X.reshape(B, C, N_PATCHES, PATCH, N_PATCHES, PATCH)
        patches = patches.transpose(0, 2, 4, 1, 3, 5).reshape(B, N_PATCHES * N_PATCHES, IN_D)
        tokens = jnp.einsum('bpi,hi->bph', patches, W) + b
        cls = jnp.broadcast_to(class_token[None, :, :], (B, 1, HID))
        tokens = jnp.concatenate([cls, tokens], axis=1)
        return tokens * pos_embed[None, :, :]

    def _L0_attn_ref(x, in_proj_w, conv_w, conv_b, x_proj_w, dt_proj_w, dt_proj_b, A_log, Dp, out_proj_w, mha_in_w, mha_in_b, mha_out_w, mha_out_b, ln1_g, ln1_b, ln2_g, ln2_b, ln3_g, ln3_b, w1, b1, w2, b2):
        import jax, jax.numpy as jnp
        import numpy as np
        D_MODEL = 128
        N_STATE = 16
        N_HEADS = 8
        D_INNER = 2 * D_MODEL
        D_CONV = 4
        DT_RANK = D_MODEL // 16
        B = 4
        L = 256
        HEAD_DIM = D_MODEL // N_HEADS

        def _ln(x, g, b):
            m = x.mean(-1, keepdims=True)
            v = ((x - m) ** 2).mean(-1, keepdims=True)
            return (x - m) / jnp.sqrt(v + 1e-05) * g + b

        def _mamba(x, in_proj_w, conv_w, conv_b, x_proj_w, dt_proj_w, dt_proj_b, A_log, Dp, out_proj_w):
            b = x.shape[0]
            xz = x @ in_proj_w.T
            u, z = jnp.split(xz, 2, axis=-1)
            uc = jax.lax.conv_general_dilated(u.transpose(0, 2, 1), conv_w, (1,), [(D_CONV - 1, 0)], dimension_numbers=('NCH', 'OIH', 'NCH'), feature_group_count=D_INNER)
            u = jax.nn.silu((uc + conv_b[None, :, None]).transpose(0, 2, 1))
            x_dbl = u @ x_proj_w.T
            dt = jax.nn.softplus(x_dbl[..., :DT_RANK] @ dt_proj_w.T + dt_proj_b)
            Bs = x_dbl[..., DT_RANK:DT_RANK + N_STATE]
            Cs = x_dbl[..., DT_RANK + N_STATE:]
            A = -jnp.exp(A_log)

            def step(h, t):
                dt_t, B_t, C_t, u_t = t
                h = jnp.exp(dt_t[:, :, None] * A) * h + (dt_t * u_t)[:, :, None] * B_t[:, None, :]
                return (h, jnp.einsum('bdn,bn->bd', h, C_t))
            h0 = jnp.zeros((b, D_INNER, N_STATE), x.dtype)
            _, ys = jax.lax.scan(step, h0, (dt.transpose(1, 0, 2), Bs.transpose(1, 0, 2), Cs.transpose(1, 0, 2), u.transpose(1, 0, 2)))
            y = ys.transpose(1, 0, 2) + u * Dp
            return y * jax.nn.silu(z) @ out_proj_w.T

        def _forward(x, in_proj_w, conv_w, conv_b, x_proj_w, dt_proj_w, dt_proj_b, A_log, Dp, out_proj_w, mha_in_w, mha_in_b, mha_out_w, mha_out_b, ln1_g, ln1_b, ln2_g, ln2_b, ln3_g, ln3_b, w1, b1, w2, b2):
            b, l, d = x.shape
            m = _mamba(x, in_proj_w, conv_w, conv_b, x_proj_w, dt_proj_w, dt_proj_b, A_log, Dp, out_proj_w)
            h1 = _ln(m + x, ln1_g, ln1_b)
            qkv = h1 @ mha_in_w.T + mha_in_b
            q, k, v = [t.reshape(b, l, N_HEADS, HEAD_DIM).transpose(0, 2, 1, 3) for t in jnp.split(qkv, 3, axis=-1)]
            s = jnp.einsum('bhqd,bhkd->bhqk', q, k) * (1.0 / float(np.sqrt(HEAD_DIM)))
            o = jnp.einsum('bhqk,bhkd->bhqd', jax.nn.softmax(s, axis=-1), v)
            attn = o.transpose(0, 2, 1, 3).reshape(b, l, d) @ mha_out_w.T + mha_out_b
            h2 = _ln(attn + h1, ln2_g, ln2_b)
            ff = jax.nn.gelu(h2 @ w1.T + b1, approximate=False) @ w2.T + b2
            return _ln(ff + h2, ln3_g, ln3_b)
        return _forward(x, in_proj_w, conv_w, conv_b, x_proj_w, dt_proj_w, dt_proj_b, A_log, Dp, out_proj_w, mha_in_w, mha_in_b, mha_out_w, mha_out_b, ln1_g, ln1_b, ln2_g, ln2_b, ln3_g, ln3_b, w1, b1, w2, b2)

    def _L0_ffn_ref(x, Wg, bg, We, be):
        import jax, jax.numpy as jnp
        import numpy as np
        B, S, D, E, O = (256, 64, 128, 16, 128)
        scores = jax.nn.softmax(jnp.mean(x, axis=1) @ Wg + bg, axis=-1)
        idx = jnp.argmax(scores, axis=-1)
        gate = jnp.take_along_axis(scores, idx[:, None], axis=-1)
        W_sel = We[idx]
        b_sel = be[idx]
        y = jnp.einsum('bsd,bdo->bso', x, W_sel) + b_sel[:, None, :]
        return gate[:, :, None] * y
    h = _L0_tok_ref(x, L0_tok_W, L0_tok_b, L0_tok_class_token, L0_tok_pos_embed)
    h = jnp.concatenate([h, txt], axis=1)
    h = h + _L0_attn_ref(_layernorm(h, axis=-1), L0_attn_in_proj_w, L0_attn_conv_w, L0_attn_conv_b, L0_attn_x_proj_w, L0_attn_dt_proj_w, L0_attn_dt_proj_b, L0_attn_A_log, L0_attn_Dp, L0_attn_out_proj_w, L0_attn_mha_in_w, L0_attn_mha_in_b, L0_attn_mha_out_w, L0_attn_mha_out_b, L0_attn_ln1_g, L0_attn_ln1_b, L0_attn_ln2_g, L0_attn_ln2_b, L0_attn_ln3_g, L0_attn_ln3_b, L0_attn_w1, L0_attn_b1, L0_attn_w2, L0_attn_b2)
    h = h + _L0_ffn_ref(_layernorm(h, axis=-1), L0_ffn_Wg, L0_ffn_bg, L0_ffn_We, L0_ffn_be)
    return h

_drawn_inputs = setup_inputs


def setup_inputs(seed=0):
    import zlib

    import numpy as np

    out = dict(_drawn_inputs(seed))
    spreads = {'L0_attn_conv_b': (0.0, 0.8),
     'L0_attn_Dp': (1.0, 0.6),
     'L0_attn_mha_in_b': (0.0, 0.52),
     'L0_attn_mha_out_b': (0.0, 0.1),
     'L0_attn_ln1_g': (1.0, 0.2),
     'L0_attn_ln1_b': (0.0, 0.1),
     'L0_attn_ln2_g': (1.0, 0.2),
     'L0_attn_ln2_b': (0.0, 0.1),
     'L0_attn_ln3_g': (1.0, 0.2),
     'L0_attn_ln3_b': (0.0, 0.1),
     'L0_attn_b1': (0.0, 0.429),
     'L0_attn_b2': (0.0, 0.1)}
    factors = {'L0_tok_b': 4.971,
     'L0_attn_in_proj_w': 8.0,
     'L0_attn_conv_w': 8.0,
     'L0_attn_x_proj_w': 8.0,
     'L0_attn_dt_proj_w': 8.0,
     'L0_attn_dt_proj_b': 8.0,
     'L0_attn_A_log': 8.0,
     'L0_attn_out_proj_w': 8.0,
     'L0_attn_mha_in_w': 8.0,
     'L0_attn_mha_out_w': 3.596,
     'L0_ffn_bg': 5.601,
     'L0_ffn_be': 8.0}
    for name, (base, spread) in spreads.items():
        noise = np.random.default_rng([zlib.crc32(name.encode()), seed]).standard_normal(out[name].shape)
        drawn = base * np.exp(spread * noise) if base else spread * noise
        out[name] = jnp.asarray(drawn.astype(out[name].dtype))
    for name, factor in factors.items():
        out[name] = (out[name] * factor).astype(out[name].dtype)
    return out
```

```python
from contextlib import ExitStack

import numpy as np

import concourse.bass as bass
from concourse import mybir

F32 = mybir.dt.float32
U32 = mybir.dt.uint32
ALU = mybir.AluOpType
ACT = mybir.ActivationFunctionType
AX = mybir.AxisListType

B, C_IN, IMG, PATCH = 64, 3, 224, 28
GRID = IMG // PATCH
NPATCH = GRID * GRID
NIMG = NPATCH + 1
NTXT = 128
T = NIMG + NTXT
D = 128
DI = 256
H2 = DI // 128
NS = 16
TAPS = 4
RANK = 8
HEADS, HD = 8, 16
QUAD = 32
GRP = HEADS // 4
FF = 4 * D
FC = FF // 128
E = 16
PAIR = 2
NP = B // PAIR
W = PAIR * T
IN_D = C_IN * PATCH * PATCH
KP = 112
KT = IN_D // KP
NG = 4
CH = NS // NG
NCH = H2 * CH
KTILES = ((0, 128), (128, T - 128))
EPS = 1e-5
SMALL = 1 / 32

COLS = {}
for _n, _w in (("tok_b", 1), ("cls", 1), ("pos", NIMG), ("conv_w", H2 * TAPS), ("conv_b", H2), ("a_log", H2 * NS),
               ("dp", H2), ("bq", GRP), ("bk", GRP), ("bv", GRP), ("bo", 1), ("g1", 1), ("e1", 1), ("g2", 1),
               ("e2", 1), ("g3", 1), ("e3", 1), ("b1", FC), ("b2", 1)):
    COLS[_n] = (sum(w for _, w in COLS.values()), _w)
NCOL = sum(w for _, w in COLS.values())


def fusion_kernel(nc, xh, txt, cols, tokw, inw, xw, dtw, outw, qkw, vw, ow, w1, w2, wg, bgrow, wexp, ident, out):
    bc_dram = nc.dram_tensor("bc_scratch", [2 * NS, W], F32, kind="Internal").ap()
    with ExitStack() as ctx:
        def sb(name, shape, dt=F32):
            return ctx.enter_context(nc.sbuf_tensor(name, shape, dt))

        def sem(name):
            return ctx.enter_context(nc.semaphore(name))

        colt = sb("colt", [128, NCOL])
        tokw_s = sb("tokw_s", [KP, KT, D])
        inw_s = sb("inw_s", [128, 4, 128])
        xw_s = sb("xw_s", [128, H2, 64])
        dtw_s = sb("dtw_s", [RANK + 1, H2, 128])
        outw_s = sb("outw_s", [128, H2, 128])
        qkw_s = sb("qkw_s", [128, 2 * GRP, 128])
        vw_s = sb("vw_s", [128, D])
        ow_s = sb("ow_s", [128, GRP, D])
        w1_s = sb("w1_s", [128, FC, 128])
        w2_s = sb("w2_s", [128, FC, D])
        wg_s = sb("wg_s", [128, E])
        bg_s = sb("bg_s", [1, PAIR, E])
        wexp_s = sb("wexp_s", [128, E * (D + 1)])
        ident_s = sb("ident_s", [128, 128])
        mean_w = sb("mean_w", [128, 128])
        ones_s = sb("ones_s", [128, 128])
        eps_s = sb("eps_s", [128, 1])
        zero_s = sb("zero_s", [128, 1])
        neg_small = sb("neg_small", [128, 1])
        one_small = sb("one_small", [128, 1])
        ln_small = sb("ln_small", [128, 1])
        a_neg = sb("a_neg", [128, H2 * NS])
        bo_all = sb("bo_all", [128, 1])

        def col(name, i=0, n=1):
            o = COLS[name][0] + i
            return colt[:, o:o + n]

        x_t = sb("x_t", [KP, KT, PAIR * NPATCH])
        h_new = sb("h_new", [128, PAIR, T])
        h_mid = sb("h_mid", [128, PAIR, T])
        cen0 = sb("cen0", [128, W])
        sq0 = sb("sq0", [128, W])
        rstd0 = sb("rstd0", [128, W])
        x0 = sb("x0", [128, W])
        u_pad = sb("u_pad", [128, H2 * PAIR, T + TAPS - 1])
        cv = sb("cv", [128, H2 * PAIR, T])
        th = sb("th", [128, H2, W])
        u = sb("u", [128, H2, W])
        zt = sb("zt", [128, H2, W])
        zs = sb("zs", [128, H2, W])
        xd = sb("xd", [64, W])
        dt = sb("dt", [128, H2, W])
        dtu = sb("dtu", [128, H2, W])
        bc_rep = sb("bc_rep", [128, 2, 2, NG, W])
        dec = sb("dec", [128, 2, NG, PAIR, T])
        drv = sb("drv", [128, 2, NG, W])
        hst = sb("hst", [128, 2, NG, W])
        hsum = sb("hsum", [128, 2, NG // 2, W])
        ypd = sb("ypd", [128, H2, W])
        sp_e, sp_l = ypd, th
        sp_p = sb("sp_p", [128, H2, W])
        sp_c = sb("sp_c", [128, H2, W])
        r1 = sb("r1", [128, W])
        h_res = sb("h_res", [128, PAIR, T])
        cen = sb("cen", [128, W])
        sq = sb("sq", [128, W])
        rstd = sb("rstd", [128, W])
        h1 = sb("h1", [128, W])
        qT = sb("qT", [128, GRP, W])
        kT = sb("kT", [128, GRP, W])
        v_s = sb("v_s", [128, PAIR, 2, HEADS, QUAD])
        negm = sb("negm", [128, 2, GRP, 4, QUAD])
        pT = sb("pT", [128, 2, HEADS, T])
        rden = sb("rden", [128, GRP, T])
        oT = sb("oT", [128, GRP, PAIR, T])
        r2 = sb("r2", [128, W])
        h2 = sb("h2", [128, W])
        hid = sb("hid", [128, FC, W])
        hh = sb("hh", [128, W])
        xm = sb("xm", [128, PAIR, T])
        msum = sb("msum", [128, PAIR])
        lg = sb("lg", [1, PAIR, E])
        top8 = sb("top8", [1, PAIR, 8])
        idx8 = sb("idx8", [1, PAIR, 8], U32)
        top_seen = sb("top_seen", [1, PAIR, 8])
        lgm = sb("lgm", [1, PAIR, E])
        lge = sb("lge", [1, PAIR, E])
        den2 = sb("den2", [1, PAIR])
        gate = sb("gate", [1, PAIR])
        gate_b = sb("gate_b", [128, PAIR])
        wsel = sb("wsel", [128, PAIR, D + 1])
        outb = sb("outb", [128, PAIR, T])

        mp = ctx.enter_context(nc.psum_tensor("mp", [128, 4, 512], F32))
        rp = ctx.enter_context(nc.psum_tensor("rp", [128, 4, 512], F32))

        s = {n: sem(n) for n in (
            "consts_in", "preset_done", "a_exp", "a_done", "halves_done", "bvo_mm", "prep_done",
            "x_in", "txt_in", "tok_mm", "tok_done",
            "hmid_done", "hres_done",
            "ln0_mean", "ln0_cen", "ln0_sq", "ln0_var", "ln0_lnv", "ln0_rstd", "ln0_out",
            "in_mm", "u_evac", "zt_done", "zs_done", "conv_step", "th_done", "u_done",
            "xp_mm", "xd_evac", "bc_out", "bc_in0", "bc_in1", "dt_mm", "sp_step", "lp_step", "dt_done", "dtu_done",
            "dec_done", "drv_done", "scan_done", "hc_done", "hsum_done", "y_mm", "ypd_done", "g_done",
            "op_mm", "r1_done",
            "qk_mm", "q_done", "k_done", "v_mm", "v_done", "s_mm", "max_done", "mt_mm", "qaug_done",
            "st_mm", "p_done", "pv_mm", "rden_done", "o_done", "ao_mm", "r2_done",
            "f1_mm", "gelu_done", "f2_mm", "r3_done", "hh_done", "msum_done", "lg_mm", "lg_done",
            "top_done", "idx_done", "lgm_done", "lge_done", "den_done", "gate_done", "gb_mm", "gb_done",
            "wsel_done", "y2_mm", "outb_part", "outb_done", "out_stored")}
        for k in range(1, 5):
            for n in ("mean", "cen", "sq", "var", "lnv", "rstd", "nrm", "out"):
                s[f"ln{k}_{n}"] = sem(f"ln{k}_{n}")

        def need(eng, name, count):
            if not isinstance(count, int) or count > 0:
                eng.wait_ge(s[name], count)

        def apart(eng):
            eng.wait_ge(s["consts_in"], 16)

        consts = [(colt[:, :], cols), (tokw_s[:, :, :], tokw), (inw_s[:, :, :], inw), (xw_s[:, :, :], xw),
                  (dtw_s[:, :, :], dtw), (outw_s[:, :, :], outw), (qkw_s[:, :, :], qkw), (vw_s[:, :], vw),
                  (ow_s[:, :, :], ow), (w1_s[:, :, :], w1), (w2_s[:, :, :], w2), (wg_s[:, :], wg),
                  (bg_s[:, :, :], bgrow), (wexp_s[:, :], wexp), (ident_s[:, :], ident)]
        ALL_CONSTS = 16 * len(consts)
        PRESETS = 12

        flat = "p a b -> p (a b)"

        def run(steps, m, r, t):
            def mamba(name):
                if m is not None and name in steps:
                    steps[name](m)

            def rest(name):
                if r is not None and name in steps:
                    steps[name](r)

            mamba("ln0")
            rest("take")
            mamba("in_proj")
            rest("ln1")
            mamba("conv")
            mamba("x_proj")
            rest("qkv")
            mamba("dt")
            parts = (["att00"], ["att01", "att0b"], ["att10"], ["att11", "att1b"], ["attn_out", "ln2"], ["ffn"],
                     ["ln3", "ln4"], ["expert"])
            for c in range(NCH):
                if m is not None and "chunk" in steps:
                    steps["chunk"](m, c)
                for name in parts[c]:
                    rest(name)
            mamba("m_out")
            if t is not None and "tok" in steps:
                steps["tok"](t)

        def program(steps, eng):
            if "tok" in steps:
                steps["tok"](0)
            run(steps, 0, None, 1)
            run(steps, 1, 0, 2)
            with eng.Fori(2, NP - 1) as i:
                run(steps, i, i - 1, i + 1)
            run(steps, NP - 1, NP - 2, None)
            run(steps, None, NP - 1, None)

        block = ctx.enter_context(nc.Block())

        @block.sync
        def _(sp):
            for dst, src in consts:
                sp.dma_start(dst, src).then_inc(s["consts_in"], 16)

            def tok(t):
                need(sp, "tok_mm", t)
                sp.dma_start(x_t[:, :, :], xh[t]).then_inc(s["x_in"], 16)
                need(sp, "hmid_done", t)
                need(sp, "ln0_cen", t)
                sp.dma_start(h_new[:, :, NIMG:T], txt[t]).then_inc(s["txt_in"], 16)

            def x_proj(m):
                need(sp, "xd_evac", 2 * m + 2)
                sp.dma_start(bc_dram, xd[32:64, :]).then_inc(s["bc_out"], 16)
                need(sp, "bc_out", 16 * m + 16)
                for g in range(2):
                    spread(m, g)

            def spread(m, g):
                used = NCH * m + H2 * (g - 1)
                need(sp, "hc_done", used if not isinstance(used, int) else max(used, 0))
                need(sp, "drv_done", used if not isinstance(used, int) else max(used, 0))
                for k in range(2):
                    rows = bc_dram[k * NS + NG * g:k * NS + NG * g + NG, :]
                    sp.dma_start(bc_rep[:, g % 2, k, :, :], rows.unsqueeze(0).to_broadcast([128, NG, W])
                                 ).then_inc(s[f"bc_in{g % 2}"], 16)

            def chunk(m, c):
                if c % 2 == 1 and c // 2 + 2 < CH:
                    spread(m, c // 2 + 2)

            def expert(r):
                need(sp, "outb_done", r + 1)
                sp.dma_start(out[r], outb[:, :, :]).then_inc(s["out_stored"], 16)

            program({"tok": tok, "x_proj": x_proj, "chunk": chunk, "expert": expert}, sp)
            sp.wait_ge(s["out_stored"], 16 * NP)

        @block.gpsimd
        def _(pool):
            def copy(dst, src):
                p, n, w = src.shape
                ones = ones_s[0:p, 0:1].unsqueeze(1).to_broadcast([p, n, w])
                return pool.tensor_tensor(dst, src, ones, ALU.mult)

            def take(r):
                pool.wait_ge(s["hmid_done"], r + 1)
                need(pool, "hh_done", r)
                copy(h_res[:, :, :], h_mid[:, :, :]).then_inc(s["hres_done"], 1)

            def in_proj(m):
                pool.wait_ge(s["tok_done"], m + 1)
                pool.wait_ge(s["txt_in"], 16 * m + 16)
                need(pool, "hres_done", m)
                copy(h_mid[:, :, :], h_new[:, :, :]).then_inc(s["hmid_done"], 1)

            def chunk(m, c):
                half, g, slot = c % H2, c // H2, c % 2
                n = NCH * m + c
                if half == 0:
                    pool.wait_ge(s[f"bc_in{g % 2}"], 32 * (CH // 2 * m + g // 2 + 1))
                if c == 0:
                    pool.wait_ge(s["dtu_done"], m + 1)
                need(pool, "scan_done", n - 1 if c >= 1 else n - 1 if not isinstance(n, int) else max(n - 1, 0))
                pool.tensor_tensor(drv[:, slot, :, :], dtu[:, half:half + 1, :].to_broadcast([128, NG, W]),
                                   bc_rep[:, g % 2, 0, :, :], ALU.mult).then_inc(s["drv_done"], 1)
                if c > 0:
                    fold(m, c - 1)
                if c == NCH - 1:
                    fold(m, c)

            def fold(m, c):
                slot = c % 2
                n = NCH * m + c
                pool.wait_ge(s["hc_done"], n + 1)
                need(pool, "y_mm", n - 1 if not isinstance(n, int) else max(n - 1, 0))
                pool.tensor_tensor(hsum[:, slot, :, :], hst[:, slot, 0:2, :], hst[:, slot, 2:4, :],
                                   ALU.add).then_inc(s["hsum_done"], 1)

            def expert(r):
                pool.wait_ge(s["idx_done"], PAIR * r + PAIR)
                need(pool, "outb_part", PAIR * r)
                copy(top_seen[:, :, :], top8[:, :, :])
                for b in range(PAIR):
                    e = pool.value_load(idx8[0:1, b, 0:1], min_val=0, max_val=E - 1)
                    pool.tensor_copy(wsel[:, b, :], wexp_s[:, bass.ds(e * (D + 1), D + 1)]).then_inc(s["wsel_done"], 1)

            pool.wait_ge(s["consts_in"], ALL_CONSTS)
            pool.wait_ge(s["preset_done"], PRESETS)
            program({"take": take, "in_proj": in_proj, "chunk": chunk, "expert": expert}, pool)

        @block.scalar
        def _(act):
            A = act.activation
            act.wait_ge(s["consts_in"], ALL_CONSTS)
            act.wait_ge(s["preset_done"], PRESETS)
            A(a_neg[:, :], col("a_log", 0, H2 * NS), ACT.Exp).then_inc(s["a_exp"], 1)
            A(ln_small[:, :], zero_s[:, :], ACT.Ln, bias=one_small[:, :]).then_inc(s["a_exp"], 1)
            act.wait_ge(s["a_done"], 1)

            def norm(k, r, sq_t, cen_t, rstd_t, var_ps):
                act.wait_ge(s[f"ln{k}_cen"], r + 1)
                A(sq_t[:, :], cen_t[:, :], ACT.Square).then_inc(s[f"ln{k}_sq"], 1)
                act.wait_ge(s[f"ln{k}_var"], r + 1)
                A(rstd_t[:, :], var_ps, ACT.Ln, bias=eps_s[:, :]).then_inc(s[f"ln{k}_lnv"], 1)
                act.wait_ge(s[f"ln{k}_lnv"], r + 1)
                A(rstd_t[:, :], rstd_t[:, :], ACT.Exp, scale=-0.5).then_inc(s[f"ln{k}_rstd"], 1)

            def ln0(m):
                norm(0, m, sq0, cen0, rstd0, mp[:, 1, 0:W])

            def in_proj(m):
                act.wait_ge(s["in_mm"], 2 * m + 1)
                need(act, "conv_step", H2 * TAPS * m)
                A(u_pad[:, :, TAPS - 1:], mp[:, 0:2, 0:W].rearrange("p h (b t) -> p h b t", b=PAIR),
                  ACT.Copy).then_inc(s["u_evac"], 1)
                act.wait_ge(s["in_mm"], 2 * m + 2)
                need(act, "zs_done", m)
                A(zt[:, :, :], mp[:, 2:4, 0:W], ACT.Tanh, scale=0.5).then_inc(s["zt_done"], 1)

            def conv(m):
                act.wait_ge(s["conv_step"], H2 * TAPS * (m + 1))
                A(th[:, :, :].rearrange("p h w -> p (h w)"), cv[:, :, :].rearrange(flat),
                  ACT.Tanh).then_inc(s["th_done"], 1)

            def x_proj(m):
                act.wait_ge(s["xp_mm"], m + 1)
                need(act, "dt_mm", m)
                need(act, "bc_out", 16 * m)
                A(xd[0:RANK, :], mp[0:RANK, 0, 0:W], ACT.Copy).then_inc(s["xd_evac"], 1)
                A(xd[32:64, :], mp[32:64, 0, 0:W], ACT.Copy).then_inc(s["xd_evac"], 1)

            def dt_(m):
                v = mp[:, 1:3, 0:W]
                act.wait_ge(s["dt_mm"], m + 1)
                need(act, "dt_done", m)
                A(sp_e[:, :, :], v, ACT.Abs).then_inc(s["sp_step"], 1)
                act.wait_ge(s["sp_step"], 4 * m + 1)
                A(sp_e[:, :, :], sp_e[:, :, :], ACT.Exp, scale=-1.0).then_inc(s["sp_step"], 1)
                act.wait_ge(s["sp_step"], 4 * m + 2)
                A(sp_l[:, :, :], sp_e[:, :, :], ACT.Relu, bias=neg_small[:, :]).then_inc(s["sp_step"], 1)
                act.wait_ge(s["sp_step"], 4 * m + 3)
                A(sp_l[:, :, :], sp_l[:, :, :], ACT.Ln, bias=one_small[:, :]).then_inc(s["sp_step"], 1)

            def chunk(m, c):
                half, g, slot = c % H2, c // H2, c % 2
                n = NCH * m + c
                if c == 0:
                    act.wait_ge(s["dt_done"], m + 1)
                need(act, "scan_done", n - 1 if not isinstance(n, int) else max(n - 1, 0))
                src = dt[:, half, :].rearrange("p (b t) -> p b t", b=PAIR)[:, :, 1:T]
                for j in range(NG):
                    k = half * NS + g * NG + j
                    last = A(dec[:, slot, j, :, 1:T], src, ACT.Exp, scale=a_neg[:, k:k + 1])
                last.then_inc(s["dec_done"], 1)

            def ln(k):
                return lambda r: norm(k, r, sq, cen, rstd, rp[:, 1, 0:W])

            def qkv(r):
                act.wait_ge(s["qk_mm"], r + 1)
                need(act, "st_mm", 4 * r)
                for g in range(GRP):
                    last = A(kT[:, g, :], rp[:, 2 + g, 0:W], ACT.Identity, bias=col("bk", g))
                last.then_inc(s["k_done"], 1)
                act.wait_ge(s["v_mm"], r + 1)
                need(act, "pv_mm", PAIR * r)
                for t, (_, n) in enumerate(KTILES):
                    last = A(v_s[0:n, :, t, :, 0:HD],
                             rp[0:n, 0, 0:512].rearrange("p (b t h e) -> p b t h e", b=PAIR, t=2, h=HEADS)[:, :, t],
                             ACT.Copy)
                last.then_inc(s["v_done"], 1)

            def probs(b):
                def f(r):
                    need(act, "pv_mm", PAIR * r + b)
                    for t, (_, n) in enumerate(KTILES):
                        act.wait_ge(s["st_mm"], 4 * r + 2 * b + t + 1)
                        A(pT[0:n, t, :, :].rearrange("p (g e) q -> p g (e q)", g=4), rp[0:n, :, 0:W],
                          ACT.Exp).then_inc(s["p_done"], 1)
                return f

            def ffn(r):
                need(act, "f2_mm", r)
                for j in range(FC):
                    act.wait_ge(s["f1_mm"], FC * r + j + 1)
                    A(hid[:, j, :], rp[:, j, 0:W], ACT.Gelu, bias=col("b1", j)).then_inc(s["gelu_done"], 1)

            def expert(r):
                act.wait_ge(s["lgm_done"], PAIR * r + PAIR)
                A(lge[:, :, :], lgm[:, :, :], ACT.Exp).then_inc(s["lge_done"], 1)

            program({"ln0": ln0, "in_proj": in_proj, "conv": conv, "x_proj": x_proj, "dt": dt_, "chunk": chunk,
                     "ln1": ln(1), "qkv": qkv, "att0b": probs(0), "att1b": probs(1), "ln2": ln(2), "ffn": ffn,
                     "ln3": ln(3), "ln4": ln(4), "expert": expert}, act)

        @block.tensor
        def _(pe):
            def mm(out_ps, lhsT, rhs, first=True, last=True):
                return pe.matmul(out_ps, lhsT, rhs, start=first, stop=last)

            pe.wait_ge(s["consts_in"], ALL_CONSTS)
            pe.wait_ge(s["halves_done"], 2)
            for g in range(GRP):
                last = mm(rp[:, 0, 0:1], ow_s[:, g, :], col("bv", g), g == 0, g == GRP - 1)
            last.then_inc(s["bvo_mm"], 1)
            pe.wait_ge(s["prep_done"], 1)

            def tok(t):
                pe.wait_ge(s["x_in"], 16 * t + 16)
                need(pe, "dt_done", t)
                for k in range(KT):
                    last = mm(mp[:, 1, 0:PAIR * NPATCH], tokw_s[:, k, :], x_t[:, k, :], k == 0, k == KT - 1)
                last.then_inc(s["tok_mm"], 1)

            def ln0(m):
                pe.wait_ge(s["tok_done"], m + 1)
                pe.wait_ge(s["txt_in"], 16 * m + 16)
                need(pe, "r1_done", m)
                mm(mp[:, 0, 0:W], mean_w[:, :], h_new[:, :, :].rearrange(flat)).then_inc(s["ln0_mean"], 1)
                pe.wait_ge(s["ln0_sq"], m + 1)
                mm(mp[:, 1, 0:W], mean_w[:, :], sq0[:, :]).then_inc(s["ln0_var"], 1)

            def in_proj(m):
                pe.wait_ge(s["ln0_out"], m + 1)
                for j in range(4):
                    last = mm(mp[:, j, 0:W], inw_s[:, j, :], x0[:, :])
                    if j % 2 == 1:
                        last.then_inc(s["in_mm"], 1)

            def x_proj(m):
                pe.wait_ge(s["u_done"], m + 1)
                for h in range(H2):
                    last = mm(mp[0:64, 0, 0:W], xw_s[:, h, :], u[:, h, :], h == 0, h == H2 - 1)
                last.then_inc(s["xp_mm"], 1)

            def dt_(m):
                pe.wait_ge(s["xd_evac"], 2 * m + 1)
                for h in range(H2):
                    last = mm(mp[:, 1 + h, 0:W], dtw_s[:, h, :], xd[0:RANK + 1, :])
                last.then_inc(s["dt_mm"], 1)

            def chunk(m, c):
                def sums(c):
                    half, g, slot = c % H2, c // H2, c % 2
                    pe.wait_ge(s["hsum_done"], NCH * m + c + 1)
                    for j in range(NG // 2):
                        last = mm(mp[:, 3 - half, 0:W], ident_s[:, :], hsum[:, slot, j, :], g == 0 and j == 0,
                                  g == CH - 1 and j == NG // 2 - 1)
                    last.then_inc(s["y_mm"], 1)
                if c > 0:
                    sums(c - 1)
                if c == NCH - 1:
                    sums(c)

            def m_out(m):
                pe.wait_ge(s["g_done"], m + 1)
                for h in range(H2):
                    last = mm(mp[:, 0, 0:W], outw_s[:, h, :], ypd[:, h, :], h == 0, h == H2 - 1)
                last.then_inc(s["op_mm"], 1)

            def ln(k, src, ready):
                def f(r):
                    pe.wait_ge(s[ready], r + 1)
                    if k == 1:
                        need(pe, "outb_part", PAIR * r)
                    mm(rp[:, 0, 0:W], mean_w[:, :], src).then_inc(s[f"ln{k}_mean"], 1)
                    pe.wait_ge(s[f"ln{k}_sq"], r + 1)
                    mm(rp[:, 1, 0:W], mean_w[:, :], sq[:, :]).then_inc(s[f"ln{k}_var"], 1)
                return f

            def qkv(r):
                pe.wait_ge(s["ln1_out"], r + 1)
                for g in range(2 * GRP):
                    last = mm(rp[:, g, 0:W], qkw_s[:, g, :], h1[:, :])
                last.then_inc(s["qk_mm"], 1)
                pe.wait_ge(s["q_done"], GRP * r + GRP)
                for b in range(PAIR):
                    for t, (k0, n) in enumerate(KTILES):
                        o = (2 * b + t) * D
                        last = mm(rp[0:n, 0, o:o + D], h1[:, b * T + k0:b * T + k0 + n], vw_s[:, :])
                last.then_inc(s["v_mm"], 1)

            def scores(b, t):
                k0, n = KTILES[t]

                def f(r):
                    pe.wait_ge(s["k_done"], r + 1)
                    pe.wait_ge(s["v_done"], r + 1)
                    if t:
                        pe.wait_ge(s["max_done"], 4 * r + 2 * b + 1)
                    elif b:
                        pe.wait_ge(s["o_done"], PAIR * r + 1)
                    for e in range(GRP):
                        for g in range(4):
                            rows = slice(QUAD * g, QUAD * g + HD)
                            last = mm(rp[0:n, g, e * T:e * T + T], qT[rows, e, b * T + k0:b * T + k0 + n],
                                      kT[rows, e, b * T:b * T + T])
                    last.then_inc(s["s_mm"], 1)
                return f

            def attend(b):
                def f(r):
                    pe.wait_ge(s["max_done"], 4 * r + 2 * b + 2)
                    for e in range(GRP):
                        for t, (k0, n) in enumerate(KTILES):
                            last = pe.transpose(rp[:, 0, e * T + k0:e * T + k0 + n],
                                                negm[0:n, t, e, :, :].rearrange(flat), ident_s[0:n, 0:n])
                    last.then_inc(s["mt_mm"], 1)
                    pe.wait_ge(s["qaug_done"], PAIR * r + b + 1)
                    for t, (k0, n) in enumerate(KTILES):
                        if t:
                            pe.wait_ge(s["p_done"], 4 * r + 2 * b + 1)
                        for e in range(GRP):
                            for g in range(4):
                                rows = slice(QUAD * g, QUAD * g + HD + 1)
                                last = mm(rp[0:n, g, e * T:e * T + T], kT[rows, e, b * T + k0:b * T + k0 + n],
                                          qT[rows, e, b * T:b * T + T])
                        last.then_inc(s["st_mm"], 1)
                    pe.wait_ge(s["p_done"], 4 * r + 2 * b + 2)
                    for bank in (0, 1):
                        for e in range(GRP):
                            for t, (_, n) in enumerate(KTILES):
                                for g in range(4):
                                    head = GRP * g + e
                                    lhsT = v_s[0:n, b, t, head_at(g, e), :] if bank == 0 else ones_s[0:n, 0:QUAD]
                                    last = mm(rp[QUAD * g:QUAD * g + QUAD, bank, e * T:e * T + T], lhsT,
                                              pT[0:n, t, head, :], t == 0, t == 1)
                    last.then_inc(s["pv_mm"], 1)
                return f

            def head_at(g, e):
                return 4 * e + g

            def attn_out(r):
                pe.wait_ge(s["o_done"], PAIR * r + PAIR)
                for g in range(GRP):
                    last = mm(rp[:, 0, 0:W], ow_s[:, g, :], oT[:, g, :, :].rearrange(flat), g == 0, g == GRP - 1)
                last.then_inc(s["ao_mm"], 1)

            def ffn(r):
                pe.wait_ge(s["ln2_out"], r + 1)
                for j in range(FC):
                    mm(rp[:, j, 0:W], w1_s[:, j, :], h2[:, :]).then_inc(s["f1_mm"], 1)
                for j in range(FC):
                    pe.wait_ge(s["gelu_done"], FC * r + j + 1)
                    last = mm(rp[:, 0, 0:W], w2_s[:, j, :], hid[:, j, :], j == 0, j == FC - 1)
                last.then_inc(s["f2_mm"], 1)

            def expert(r):
                pe.wait_ge(s["msum_done"], r + 1)
                for b in range(PAIR):
                    last = mm(rp[0:1, 0, b * E:b * E + E], msum[:, b:b + 1], wg_s[:, :])
                last.then_inc(s["lg_mm"], 1)
                pe.wait_ge(s["gate_done"], r + 1)
                mm(rp[:, 1, 0:PAIR], ones_s[0:1, :], gate[:, :]).then_inc(s["gb_mm"], 1)
                pe.wait_ge(s["wsel_done"], PAIR * r + PAIR)
                for b in range(PAIR):
                    last = mm(rp[:, 2, b * T:b * T + T], wsel[:, b, 0:D], xm[:, b, :])
                last.then_inc(s["y2_mm"], 1)

            program({"tok": tok, "ln0": ln0, "in_proj": in_proj, "x_proj": x_proj, "dt": dt_, "chunk": chunk,
                     "m_out": m_out, "ln1": ln(1, r1[:, :], "r1_done"), "qkv": qkv,
                     "att00": scores(0, 0), "att01": scores(0, 1), "att0b": attend(0),
                     "att10": scores(1, 0), "att11": scores(1, 1), "att1b": attend(1),
                     "attn_out": attn_out, "ln2": ln(2, r2[:, :], "r2_done"), "ffn": ffn,
                     "ln3": ln(3, r2[:, :], "r3_done"), "ln4": ln(4, hh[:, :], "hh_done"), "expert": expert}, pe)

        @block.vector
        def _(dve):
            V = dve

            def stt(out_, in0, scalar, in1, op0, op1):
                return V.scalar_tensor_tensor(out=out_, in0=in0, scalar=scalar, in1=in1, op0=op0, op1=op1)

            for t_, val in ((mean_w[:, :], 1.0 / D), (ones_s[:, :], 1.0), (eps_s[:, :], EPS),
                            (zero_s[:, :], 0.0), (neg_small[:, :], -SMALL), (one_small[:, :], 1.0 + SMALL),
                            (u_pad[:, :, 0:TAPS - 1], 0.0), (dec[:, :, :, :, 0:1], 0.0), (xd[0:32, :], 1.0),
                            (v_s[:, :, :, :, HD:QUAD], 0.0), (negm[:, :, :, :, :], 0.0)):
                V.memset(t_, val).then_inc(s["preset_done"], 1)
            V.wait_ge(s["consts_in"], ALL_CONSTS)
            for b in range(PAIR):
                last = V.tensor_tensor(h_new[:, b, 0:1], col("cls"), col("pos"), ALU.mult)
            last.then_inc(s["preset_done"], 1)
            c0 = COLS["conv_w"][0]
            cw = colt[:, c0:c0 + H2 * TAPS + H2]
            V.tensor_scalar(cw, cw, 0.5, None, ALU.mult).then_inc(s["halves_done"], 1)
            V.tensor_scalar(outw_s[:, :, :], outw_s[:, :, :], 0.5, None, ALU.mult).then_inc(s["halves_done"], 1)
            V.wait_ge(s["a_exp"], 2)
            V.tensor_scalar(a_neg[:, :], a_neg[:, :], -1.0, None, ALU.mult).then_inc(s["a_done"], 1)
            V.wait_ge(s["bvo_mm"], 1)
            V.tensor_tensor(bo_all[:, :], rp[:, 0, 0:1], col("bo"), ALU.add).then_inc(s["prep_done"], 1)
            V.wait_ge(s["preset_done"], PRESETS)
            V.wait_ge(s["prep_done"], 1)

            def tok(t):
                V.wait_ge(s["tok_mm"], t + 1)
                need(V, "hmid_done", t)
                pos = col("pos", 1, NPATCH).unsqueeze(1).to_broadcast([128, PAIR, NPATCH])
                stt(h_new[:, :, 1:NIMG], mp[:, 1, 0:PAIR * NPATCH].rearrange("p (b n) -> p b n", b=PAIR),
                    col("tok_b"), pos, ALU.add, ALU.mult).then_inc(s["tok_done"], 1)

            def ln0(m):
                V.wait_ge(s["ln0_mean"], m + 1)
                V.tensor_tensor(cen0[:, :], h_new[:, :, :].rearrange(flat), mp[:, 0, 0:W],
                                ALU.subtract).then_inc(s["ln0_cen"], 1)
                V.wait_ge(s["ln0_rstd"], m + 1)
                V.tensor_tensor(x0[:, :], cen0[:, :], rstd0[:, :], ALU.mult).then_inc(s["ln0_out"], 1)

            def conv(m):
                V.wait_ge(s["u_evac"], m + 1)
                for k in range(TAPS):
                    for h in range(H2):
                        w = col("conv_w", h * TAPS + k)
                        src = u_pad[:, PAIR * h:PAIR * h + PAIR, k:k + T]
                        dst = cv[:, PAIR * h:PAIR * h + PAIR, :]
                        if k == 0:
                            V.tensor_scalar(dst, src, w, col("conv_b", h), ALU.mult,
                                            ALU.add).then_inc(s["conv_step"], 1)
                        else:
                            V.wait_ge(s["conv_step"], H2 * TAPS * m + H2 * (k - 1) + h + 1)
                            stt(dst, src, w, dst, ALU.mult, ALU.add).then_inc(s["conv_step"], 1)
                V.wait_ge(s["zt_done"], m + 1)
                need(V, "g_done", m)
                stt(zs[:, :, :], zt[:, :, :], 1.0, mp[:, 2:4, 0:W], ALU.add, ALU.mult).then_inc(s["zs_done"], 1)
                V.wait_ge(s["th_done"], m + 1)
                stt(u[:, :, :].rearrange(flat), th[:, :, :].rearrange(flat), 1.0, cv[:, :, :].rearrange(flat),
                    ALU.add, ALU.mult).then_inc(s["u_done"], 1)

            def dt_(m):
                V.wait_ge(s["sp_step"], 4 * m + 2)
                c, p = sp_c[:, :, :], sp_p[:, :, :]
                V.tensor_scalar(c, sp_e[:, :, :], SMALL, None, ALU.min).then_inc(s["lp_step"], 1)
                V.wait_ge(s["lp_step"], 6 * m + 1)
                V.tensor_scalar(p, c, -1 / 4, 1 / 3, ALU.mult, ALU.add).then_inc(s["lp_step"], 1)
                V.wait_ge(s["lp_step"], 6 * m + 2)
                V.tensor_tensor(p, p, c, ALU.mult).then_inc(s["lp_step"], 1)
                V.wait_ge(s["lp_step"], 6 * m + 3)
                stt(p, p, -1 / 2, c, ALU.add, ALU.mult).then_inc(s["lp_step"], 1)
                V.wait_ge(s["lp_step"], 6 * m + 4)
                stt(p, p, 1.0, c, ALU.add, ALU.mult).then_inc(s["lp_step"], 1)
                V.wait_ge(s["lp_step"], 6 * m + 5)
                V.wait_ge(s["sp_step"], 4 * m + 4)
                stt(p, sp_l[:, :, :], ln_small[:, :], p, ALU.subtract, ALU.add).then_inc(s["lp_step"], 1)
                V.wait_ge(s["lp_step"], 6 * m + 6)
                need(V, "drv_done", NCH * m)
                need(V, "dec_done", NCH * m)
                stt(dt[:, :, :], mp[:, 1:3, 0:W], 0.0, sp_p[:, :, :], ALU.max, ALU.add).then_inc(s["dt_done"], 1)
                V.wait_ge(s["dt_done"], m + 1)
                V.tensor_tensor(dtu[:, :, :], dt[:, :, :], u[:, :, :], ALU.mult).then_inc(s["dtu_done"], 1)

            def chunk(m, c):
                half, g, slot = c % H2, c // H2, c % 2
                n = NCH * m + c
                V.wait_ge(s["dec_done"], n + 1)
                V.wait_ge(s["drv_done"], n + 1)
                need(V, "hsum_done", n - 1 if not isinstance(n, int) else max(n - 1, 0))
                fl = hst[:, slot, :, :].rearrange(flat)
                V.tensor_tensor_scan(fl, dec[:, slot, :, :, :].rearrange("p j b t -> p (j b t)"),
                                     drv[:, slot, :, :].rearrange(flat), 0.0, ALU.mult,
                                     ALU.add).then_inc(s["scan_done"], 1)
                V.wait_ge(s["scan_done"], n + 1)
                V.tensor_tensor(fl, fl, bc_rep[:, g % 2, 1, :, :].rearrange(flat),
                                ALU.mult).then_inc(s["hc_done"], 1)

            def m_out(m):
                for h in range(H2):
                    V.wait_ge(s["y_mm"], NCH * m + NCH - 1 + h)
                    stt(ypd[:, h, :], u[:, h, :], col("dp", h), mp[:, 3 - h, 0:W], ALU.mult,
                        ALU.add).then_inc(s["ypd_done"], 1)
                V.wait_ge(s["ypd_done"], H2 * m + H2)
                V.tensor_tensor(ypd[:, :, :], ypd[:, :, :], zs[:, :, :], ALU.mult).then_inc(s["g_done"], 1)
                V.wait_ge(s["op_mm"], m + 1)
                need(V, "ln1_cen", m)
                V.tensor_tensor(r1[:, :], mp[:, 0, 0:W], x0[:, :], ALU.add).then_inc(s["r1_done"], 1)

            def ln(k, src, dst, affine=True):
                def f(r):
                    V.wait_ge(s[f"ln{k}_mean"], r + 1)
                    V.tensor_tensor(cen[:, :], src, rp[:, 0, 0:W], ALU.subtract).then_inc(s[f"ln{k}_cen"], 1)
                    V.wait_ge(s[f"ln{k}_rstd"], r + 1)
                    if not affine:
                        V.tensor_tensor(dst, cen[:, :], rstd[:, :], ALU.mult).then_inc(s[f"ln{k}_out"], 1)
                        return
                    stt(cen[:, :], cen[:, :], col(f"g{k}"), rstd[:, :], ALU.mult, ALU.mult
                        ).then_inc(s[f"ln{k}_nrm"], 1)
                    V.wait_ge(s[f"ln{k}_nrm"], r + 1)
                    V.tensor_scalar(dst, cen[:, :], col(f"e{k}"), None, ALU.add).then_inc(s[f"ln{k}_out"], 1)
                return f

            def qkv(r):
                V.wait_ge(s["qk_mm"], r + 1)
                for g in range(GRP):
                    V.tensor_scalar(qT[:, g, :], rp[:, g, 0:W], col("bq", g), HD ** -0.5, ALU.add,
                                    ALU.mult).then_inc(s["q_done"], 1)

            def maxima(b, t):
                n = KTILES[t][1]

                def f(r):
                    V.wait_ge(s["s_mm"], 4 * r + 2 * b + t + 1)
                    V.tensor_reduce(negm[0:n, t, :, :, HD].rearrange("p e g -> p g e"),
                                    rp[0:n, :, 0:W].rearrange("p g (e k) -> p g e k", e=GRP),
                                    AX.X, ALU.max, negate=True).then_inc(s["max_done"], 1)
                return f

            def attend(b):
                def f(r):
                    V.wait_ge(s["mt_mm"], PAIR * r + b + 1)
                    q = qT[:, :, b * T:b * T + T]
                    V.tensor_tensor(q, q, rp[:, 0, 0:W].rearrange("p (e k) -> p e k", e=GRP),
                                    ALU.add).then_inc(s["qaug_done"], 1)
                    V.wait_ge(s["pv_mm"], PAIR * r + b + 1)
                    V.reciprocal(rden[:, :, :].rearrange(flat), rp[:, 1, 0:W]).then_inc(s["rden_done"], 1)
                    V.wait_ge(s["rden_done"], PAIR * r + b + 1)
                    V.tensor_tensor(oT[:, :, b, :], rp[:, 0, 0:W].rearrange("p (e k) -> p e k", e=GRP),
                                    rden[:, :, :], ALU.mult).then_inc(s["o_done"], 1)
                return f

            def attn_out(r):
                V.wait_ge(s["ao_mm"], r + 1)
                stt(r2[:, :], rp[:, 0, 0:W], bo_all[:, :], h1[:, :], ALU.add, ALU.add).then_inc(s["r2_done"], 1)

            def ffn(r):
                V.wait_ge(s["f2_mm"], r + 1)
                stt(r2[:, :], rp[:, 0, 0:W], col("b2"), h2[:, :], ALU.add, ALU.add).then_inc(s["r3_done"], 1)

            def ln3(r):
                ln(3, r2[:, :], hh[:, :])(r)
                V.wait_ge(s["ln3_out"], r + 1)
                V.wait_ge(s["hres_done"], r + 1)
                V.tensor_tensor(hh[:, :], hh[:, :], h_res[:, :, :].rearrange(flat), ALU.add).then_inc(s["hh_done"], 1)

            def expert(r):
                V.wait_ge(s["ln4_out"], r + 1)
                V.tensor_reduce(msum[:, :], xm[:, :, :], AX.X, ALU.add).then_inc(s["msum_done"], 1)
                V.wait_ge(s["lg_mm"], r + 1)
                stt(lg[:, :, :], rp[0:1, 0, 0:PAIR * E].rearrange("p (b e) -> p b e", b=PAIR), 1.0 / T, bg_s[:, :, :],
                    ALU.mult, ALU.add).then_inc(s["lg_done"], 1)
                apart(V)
                V.wait_ge(s["lg_done"], r + 1)
                need(V, "wsel_done", PAIR * r)
                for b in range(PAIR):
                    V.max(top8[:, b, :], lg[:, b, :]).then_inc(s["top_done"], 1)
                for b in range(PAIR):
                    apart(V)
                    V.wait_ge(s["top_done"], PAIR * r + b + 1)
                    V.max_index(idx8[:, b, :], top8[:, b, :], lg[:, b, :]).then_inc(s["idx_done"], 1)
                    V.tensor_scalar(lgm[:, b, :], lg[:, b, :], top8[:, b, 0:1], None,
                                    ALU.subtract).then_inc(s["lgm_done"], 1)
                V.wait_ge(s["lge_done"], r + 1)
                V.tensor_reduce(den2[:, :], lge[:, :, :], AX.X, ALU.add).then_inc(s["den_done"], 1)
                V.wait_ge(s["den_done"], r + 1)
                V.reciprocal(gate[:, :], den2[:, :]).then_inc(s["gate_done"], 1)
                V.wait_ge(s["gb_mm"], r + 1)
                V.tensor_copy(gate_b[:, :], rp[:, 1, 0:PAIR]).then_inc(s["gb_done"], 1)
                V.wait_ge(s["gb_done"], r + 1)
                V.wait_ge(s["y2_mm"], r + 1)
                need(V, "out_stored", 16 * r)
                for b in range(PAIR):
                    V.tensor_scalar(outb[:, b, :], rp[:, 2, b * T:b * T + T], wsel[:, b, D:D + 1],
                                    gate_b[:, b:b + 1], ALU.add, ALU.mult).then_inc(s["outb_part"], 1)
                V.wait_ge(s["outb_part"], PAIR * r + PAIR)
                o = outb[:, :, :].rearrange(flat)
                V.tensor_tensor(o, o, hh[:, :], ALU.add).then_inc(s["outb_done"], 1)

            program({"tok": tok, "ln0": ln0, "conv": conv, "dt": dt_, "chunk": chunk, "m_out": m_out,
                     "ln1": ln(1, r1[:, :], h1[:, :]), "qkv": qkv, "att00": maxima(0, 0), "att01": maxima(0, 1),
                     "att0b": attend(0), "att10": maxima(1, 0), "att11": maxima(1, 1), "att1b": attend(1),
                     "attn_out": attn_out, "ln2": ln(2, r2[:, :], h2[:, :]), "ffn": ffn, "ln3": ln3,
                     "ln4": ln(4, hh[:, :], xm[:, :, :].rearrange(flat), affine=False), "expert": expert}, dve)


def _layout(a):
    f = np.float32

    def heads(x):
        o = np.zeros((GRP, 4, QUAD) + x.shape[1:], f)
        o[:, :, :HD] = x.reshape((GRP, 4, HD) + x.shape[1:])
        return o.reshape((GRP, 4 * QUAD) + x.shape[1:])

    x = a["x"].reshape(NP, PAIR, C_IN, GRID, PATCH, GRID, PATCH).transpose(0, 2, 4, 6, 1, 3, 5)
    lay = {"xh": x.reshape(NP, KP, KT, PAIR * NPATCH)}
    lay["txt"] = a["txt"].reshape(NP, PAIR, NTXT, D).transpose(0, 3, 1, 2)
    lay["tokw"] = a["L0_tok_W"].T.reshape(KP, KT, D)
    inw = a["L0_attn_in_proj_w"].T.reshape(D, 4, 128)
    lay["inw"] = inw
    xp = a["L0_attn_x_proj_w"]
    xw = np.zeros((64, DI), f)
    xw[0:RANK], xw[32:64] = xp[0:RANK], xp[RANK:]
    lay["xw"] = xw.T.reshape(H2, 128, 64).transpose(1, 0, 2)
    dtw = np.concatenate([a["L0_attn_dt_proj_w"].T, a["L0_attn_dt_proj_b"][None]], 0)
    lay["dtw"] = dtw.reshape(RANK + 1, H2, 128)
    lay["outw"] = a["L0_attn_out_proj_w"].T.reshape(H2, 128, D).transpose(1, 0, 2)
    qw, kw, vw = a["L0_attn_mha_in_w"].reshape(3, D, D)
    qb, kb, vb = a["L0_attn_mha_in_b"].reshape(3, D)
    lay["qkw"] = np.concatenate([heads(qw), heads(kw)], 0).transpose(2, 0, 1)
    lay["vw"] = vw.T
    lay["ow"] = heads(a["L0_attn_mha_out_w"].T).transpose(1, 0, 2)
    lay["w1"] = a["L0_attn_w1"].T.reshape(D, FC, 128)
    lay["w2"] = a["L0_attn_w2"].T.reshape(FC, 128, D).transpose(1, 0, 2)
    lay["wg"] = a["L0_ffn_Wg"]
    lay["bgrow"] = np.stack([a["L0_ffn_bg"]] * PAIR)[None]
    wexp = np.concatenate([a["L0_ffn_We"].transpose(1, 0, 2), a["L0_ffn_be"].T[:, :, None]], 2)
    lay["wexp"] = wexp.reshape(D, E * (D + 1))
    lay["ident"] = np.eye(128, dtype=f)

    def half(v):
        return v.reshape(H2, 128, -1).transpose(1, 0, 2).reshape(128, -1)

    bk = heads(kb).reshape(GRP, 4, QUAD)
    bk[:, :, HD] = 1.0
    parts = {
        "tok_b": a["L0_tok_b"], "cls": a["L0_tok_class_token"][0], "pos": a["L0_tok_pos_embed"].T,
        "conv_w": half(a["L0_attn_conv_w"]), "conv_b": half(a["L0_attn_conv_b"]), "a_log": half(a["L0_attn_A_log"]),
        "dp": half(a["L0_attn_Dp"]), "bq": heads(qb).T, "bk": bk.reshape(GRP, 128).T, "bv": heads(vb).T,
        "bo": a["L0_attn_mha_out_b"], "g1": a["L0_attn_ln1_g"], "e1": a["L0_attn_ln1_b"], "g2": a["L0_attn_ln2_g"],
        "e2": a["L0_attn_ln2_b"], "g3": a["L0_attn_ln3_g"], "e3": a["L0_attn_ln3_b"],
        "b1": a["L0_attn_b1"].reshape(FC, 128).T, "b2": a["L0_attn_b2"]}
    lay["cols"] = np.concatenate([parts[n].reshape(128, w) for n, (_, w) in COLS.items()], 1)
    return lay


_ORDER = ["xh", "txt", "cols", "tokw", "inw", "xw", "dtw", "outw", "qkw", "vw", "ow", "w1", "w2", "wg", "bgrow",
          "wexp", "ident"]


def kernel(**inputs):
    import concourse.bacc as _bacc
    from concourse.bass_utils import run_bass_kernel_spmd as _run

    lay = _layout({k: np.asarray(v) for k, v in inputs.items()})
    nc = _bacc.Bacc("TRN2", target_bir_lowering=False, num_devices=1)
    arrays, args = {}, []
    for name in _ORDER:
        arr = np.ascontiguousarray(lay[name])
        arrays[f"in_{name}"] = arr
        args.append(nc.dram_tensor(f"in_{name}", arr.shape, mybir.dt.from_np(arr.dtype), kind="ExternalInput").ap())
    args.append(nc.dram_tensor("out_0", (NP, D, PAIR, T), F32, kind="ExternalOutput").ap())
    fusion_kernel(nc, *args)
    r = _run(nc, [arrays], core_ids=[0])
    got = r.results[0]["out_0"]
    return np.ascontiguousarray(got.transpose(0, 2, 3, 1).reshape(B, T, D))
```

```python
from contextlib import ExitStack

import numpy as np

import concourse.bass as bass
from concourse import mybir

F32 = mybir.dt.float32
U32 = mybir.dt.uint32
ALU = mybir.AluOpType
ACT = mybir.ActivationFunctionType
AX = mybir.AxisListType

B, C_IN, IMG, PATCH = 64, 3, 224, 28
GRID = IMG // PATCH
NPATCH = GRID * GRID
NIMG = NPATCH + 1
NTXT = 128
T = NIMG + NTXT
D = 128
DI = 256
H2 = DI // 128
NS = 16
TAPS = 4
RANK = 8
HEADS, HD = 8, 16
QUAD = 32
GRP = HEADS // 4
FF = 4 * D
FC = FF // 128
E = 16
PAIR = 2
NP = B // PAIR
W = PAIR * T
IN_D = C_IN * PATCH * PATCH
KP = 112
KT = IN_D // KP
NG = 4
CH = NS // NG
NCH = H2 * CH
KTILES = ((0, 128), (128, T - 128))
EPS = 1e-5
SMALL = 1 / 32

COLS = {}
for _n, _w in (("tok_b", 1), ("cls", 1), ("pos", NIMG), ("conv_w", H2 * TAPS), ("conv_b", H2), ("a_log", H2 * NS),
               ("dp", H2), ("bq", GRP), ("bk", GRP), ("bv", GRP), ("bo", 1), ("g1", 1), ("e1", 1), ("g2", 1),
               ("e2", 1), ("g3", 1), ("e3", 1), ("b1", FC), ("b2", 1)):
    COLS[_n] = (sum(w for _, w in COLS.values()), _w)
NCOL = sum(w for _, w in COLS.values())

ORDER = (
    "C drv 0", "B o_ev1", "B sel1", "C dec 0", "A mean", "B rd1", "B o1", "B ao", "C scan 0", "A cen", "C dec 1",
    "F mean", "B r2", "A sq", "F cen", "C hc 0", "C drv 1", "F sq", "A var", "E2 mean", "C drv 2", "F var",
    "C fold 0", "A rstd", "E2 cen", "E2 sq", "F rstd", "E hres", "C dec 2", "E2 var", "E2 rstd", "A nrm",
    "C scan 1", "F x0", "C hc 1", "C drv 3", "A qk", "F in_u", "A qk_ev", "F u_ev", "A v", "A v_ev", "C sum 0",
    "A s00", "E2 nrm", "C dec 3", "F in_z", "F conv", "F zt", "C bc 2", "F th", "C fold 1", "C sum 1", "A max00",
    "C scan 2", "F zs", "A s01", "E f1a", "A max01", "E ga", "A mt0", "A qaug0", "C hc 2", "C scan 3", "C fold 2",
    "E f1b", "E gb", "A st00", "A pr00", "C dec 4", "E f2", "C drv 4", "E r3", "F hstore", "A st01", "C drv 5",
    "C sum 2", "C hc 3", "E3 mean", "A pr01", "E3 cen", "C dec 5", "A pv0", "F u", "F xp", "E3 sq", "A o_ev0",
    "C scan 4", "F xd", "K txt", "C bc 3", "A sel0", "C fold 3", "C sum 3", "E3 var", "C hc 4", "A rd0", "A s10",
    "C fold 4", "E3 rstd", "C drv 6", "C scan 5", "E3 nrm", "A max10", "F dt", "E hh", "C hc 5", "A s11", "A o0",
    "F sp_v", "E4 mean", "A max11", "C dec 6", "C sum 4", "A mt1", "E4 cen", "C dec 7", "E4 sq", "E4 var",
    "F sp_e", "A qaug1", "A st10", "E4 rstd", "C scan 6", "E4 xm", "C fold 5", "C sum 5", "E msum", "C hc 6",
    "A pr10", "E lg", "E top", "C drv 7", "A st11", "C scan 7", "E lge", "C fold 6", "E gate", "E gbm", "C sum 6",
    "E wsel", "A pr11", "C hc 7", "E gbc", "F bcst", "C fold 7", "K mm", "F sp_l", "C sum 7", "C y0", "F poly",
    "F bc 0", "F dtu", "K x", "E y2", "C y1", "A pv1", "C g", "E out", "C out", "F bc 1", "C r1", "E store",
    "K pos",
)
LAG = {"K": -1, "F": 0, "C": 1, "A": 2, "B": 3, "E": 3}
A_OR_B = "AB"


def fusion_kernel(nc, xh, txt, cols, tokw, inw, xw, dtw, outw, qkw, vw, ow, w1, w2, wg, bgrow, wexp, ident, spread,
                  out):
    bc_dram = nc.dram_tensor("bc_scratch", [2, 2 * NS, W], F32, kind="Internal").ap()
    h_dram = nc.dram_tensor("h_scratch", [NP, D, PAIR, T], F32, kind="Internal").ap()
    with ExitStack() as ctx:
        def sb(name, shape, dt=F32):
            return ctx.enter_context(nc.sbuf_tensor(name, shape, dt))

        def sem(name):
            return ctx.enter_context(nc.semaphore(name))

        colt = sb("colt", [128, NCOL])
        tokw_s = sb("tokw_s", [KP, KT, D])
        inw_s = sb("inw_s", [128, 4, 128])
        xw_s = sb("xw_s", [128, H2, 64])
        dtw_s = sb("dtw_s", [RANK + 1, H2, 128])
        outw_s = sb("outw_s", [128, H2, 128])
        qkw_s = sb("qkw_s", [128, 2 * GRP, 128])
        vw_s = sb("vw_s", [128, D])
        ow_s = sb("ow_s", [128, GRP, D])
        w1_s = sb("w1_s", [128, FC, 128])
        w2_s = sb("w2_s", [128, FC, D])
        wg_s = sb("wg_s", [128, E])
        bg_s = sb("bg_s", [1, PAIR, E])
        ident_s = sb("ident_s", [128, 128])
        spread_s = sb("spread_s", [128, 128])
        mean_w = sb("mean_w", [128, 128])
        ones_s = sb("ones_s", [1, 128])
        eps_s = sb("eps_s", [128, 1])
        zero_s = sb("zero_s", [128, 1])
        neg_small = sb("neg_small", [128, 1])
        unit_s = sb("unit_s", [128, 1])
        ln_unit = sb("ln_unit", [128, 1])
        a_neg = sb("a_neg", [128, H2 * NS])
        bo_all = sb("bo_all", [128, 1])

        def col(name, i=0, n=1):
            o = COLS[name][0] + i
            return colt[:, o:o + n]

        x_t = sb("x_t", [KP, KT, PAIR * NPATCH])
        h_new = sb("h_new", [128, PAIR, T])
        cen0 = sb("cen0", [128, W])
        sq0 = sb("sq0", [128, W])
        rstd0 = sq0
        x0 = sb("x0", [128, 2, W])
        u_pad = sb("u_pad", [128, H2 * PAIR, T + TAPS - 1])
        cv = sb("cv", [128, H2, W])
        th = sb("th", [128, H2, W])
        zt = sb("zt", [128, H2, W])
        sp_c, sp_l, sp_e = cv, th, zt
        xd = sb("xd", [64, W])
        u = sb("u", [128, 2, H2, W])
        zs = sb("zs", [128, 2, H2, W])
        dt = sb("dt", [128, 2, H2, W])
        dtu = sb("dtu", [128, 2, H2, W])
        bc_rep = sb("bc_rep", [128, 2, 2, NG, W])
        dec = sb("dec", [128, 2, NG, PAIR, T])
        drv = sb("drv", [128, 2, NG, W])
        hst = sb("hst", [128, 2, NG, W])
        ypd = sb("ypd", [128, H2, W])
        r1 = sb("r1", [128, W])
        cen1 = sb("cen1", [128, W])
        sq1 = sb("sq1", [128, W])
        rstd1 = sq1
        h1 = sb("h1", [128, 2, W])
        qT = sb("qT", [128, GRP, W])
        kT = sb("kT", [128, GRP, W])
        v_s = sb("v_s", [128, PAIR, 2, HEADS, QUAD])
        negm = sb("negm", [128, 2, GRP, 4, QUAD])
        pT = sb("pT", [128, 2, HEADS, T])
        o_sb = sb("o_sb", [128, GRP, T])
        rden = sb("rden", [128, GRP, T])
        oT = sb("oT", [128, GRP, PAIR, T])
        r2 = sb("r2", [128, W])
        cen = sb("cen", [128, W])
        sq = sb("sq", [128, W])
        rstd = sq
        h_res = sb("h_res", [128, PAIR, T])
        h2 = sb("h2", [128, W])
        hid = sb("hid", [128, FC, W])
        r3 = sb("r3", [128, W])
        hh = sb("hh", [128, W])
        xm = sb("xm", [128, PAIR, T])
        msum = sb("msum", [128, PAIR])
        lg = sb("lg", [1, PAIR, E])
        top8 = sb("top8", [1, PAIR, 8])
        idx8 = sb("idx8", [1, PAIR, 8], U32)
        top_seen = sb("top_seen", [1, PAIR, 8])
        lg_seen = sb("lg_seen", [1, PAIR, E])
        lgm = sb("lgm", [1, PAIR, E])
        lge = sb("lge", [1, PAIR, E])
        den2 = sb("den2", [1, PAIR])
        gate = sb("gate", [1, PAIR])
        gate_b = sb("gate_b", [128, PAIR])
        wsel = sb("wsel", [128, PAIR, D + 1])
        outb = sb("outb", [128, PAIR, T])

        fe = ctx.enter_context(nc.psum_tensor("fe", [128, 2, 512], F32))
        yp = ctx.enter_context(nc.psum_tensor("yp", [128, H2, 512], F32))
        ap = ctx.enter_context(nc.psum_tensor("ap", [128, 4, 512], F32))

        s = {n: sem(n) for n in (
            "consts_in", "preset_done", "a_exp", "a_done", "scaled_done", "bvo_mm", "prep_done",
            "x_in", "txt_in", "tok_mm", "tok_done", "h_out",
            "in_mm", "u_evac", "zt_done", "zs_done", "conv_step", "th_done", "u_done",
            "xp_mm", "xd_evac", "bc_out", "bc_in0", "bc_in1", "dt_mm", "sp_step", "lp_step", "dt_done", "dtu_done",
            "dec_done", "drv_done", "scan_done", "hc_done", "hsum_done", "hsum2_done", "y_mm", "ypd_done", "g_done",
            "op_mm", "r1_done",
            "h1_scaled", "qk_mm", "qk_done", "v_mm", "v_done", "s_mm", "max_done", "mt_mm", "qaug_done",
            "st_mm", "p_done", "pv_mm", "oev_done", "sel_mm", "rd_ln", "rd_done", "o_done", "ao_mm", "r2_done",
            "f1_mm", "gelu_done", "f2_mm", "r3_done", "hres_in", "hh_done", "msum_done", "lg_mm", "lg_done",
            "top_done", "idx_done", "top_read", "lgm_done", "lge_done", "den_done", "gate_done", "gb_mm", "gb_done",
            "wsel_in", "y2_mm", "outb_part", "outb_done", "out_stored")}
        for k in range(5):
            for n in ("mean", "cen", "sq", "var", "lnv", "rstd", "nrm", "rsq", "res", "out"):
                s[f"ln{k}_{n}"] = sem(f"ln{k}_{n}")

        def need(eng, name, count):
            if not isinstance(count, int) or count > 0:
                eng.wait_ge(s[name], count)

        def upto(pairs):
            return min(pairs, NP) if isinstance(pairs, int) else pairs

        consts = [(colt[:, :], cols), (tokw_s[:, :, :], tokw), (inw_s[:, :, :], inw), (xw_s[:, :, :], xw),
                  (dtw_s[:, :, :], dtw), (outw_s[:, :, :], outw), (qkw_s[:, :, :], qkw), (vw_s[:, :], vw),
                  (ow_s[:, :, :], ow), (w1_s[:, :, :], w1), (w2_s[:, :, :], w2), (wg_s[:, :], wg),
                  (bg_s[:, :, :], bgrow), (ident_s[:, :], ident), (spread_s[:, :], spread)]
        ALL_CONSTS = 16 * len(consts)
        PRESETS = 12

        flat = "p a b -> p (a b)"

        def iteration(steps, i, parity):
            for name in ORDER:
                lag = LAG[name[0]]
                if name not in steps or (isinstance(i, int) and not 0 <= i - lag < NP):
                    continue
                steps[name](i - lag, (parity - lag) % 2)

        def program(steps, eng):
            for i in range(-1, 4):
                iteration(steps, i, i % 2)
            with eng.Fori(2, 15) as two:
                iteration(steps, two * 2, 0)
                iteration(steps, two * 2 + 1, 1)
            for i in range(30, NP + 3):
                iteration(steps, i, i % 2)

        block = ctx.enter_context(nc.Block())

        @block.sync
        def _(sp):
            for dst, src in consts:
                sp.dma_start(dst, src).then_inc(s["consts_in"], 16)
            sp.dma_start(x_t[:, :, :], xh[0]).then_inc(s["x_in"], 16)
            sp.dma_start(h_new[:, :, NIMG:T], txt[0]).then_inc(s["txt_in"], 16)

            def waits(*counts):
                for name, count in counts:
                    sp.wait_ge(s["consts_in"], 16)
                    need(sp, name, count)

            def x_next(t, _):
                if isinstance(t, int) and t + 1 >= NP:
                    return
                waits(("tok_mm", t + 1))
                sp.dma_start(x_t[:, :, :], xh[t + 1]).then_inc(s["x_in"], 16)

            def h_store(f, _):
                waits(("tok_done", f + 1), ("txt_in", 16 * f + 16), ("h_out", 16 * f))
                sp.dma_start(h_dram[f], h_new[:, :, :]).then_inc(s["h_out"], 16)

            def txt_load(t, _):
                if isinstance(t, int) and t == 0:
                    return
                waits(("ln0_cen", t), ("h_out", 16 * t))
                sp.dma_start(h_new[:, :, NIMG:T], txt[t]).then_inc(s["txt_in"], 16)

            def bc_store(f, par):
                waits(("xd_evac", 2 * f + 2), ("drv_done", NCH * (f - 1)))
                sp.dma_start(bc_dram[par], xd[32:64, :]).then_inc(s["bc_out"], 16)

            def bc_load(g):
                def f(m, par):
                    used = NCH * m + H2 * (g - 1)
                    waits(*([("bc_out", 16 * m + 16)] if g == 0 else []), ("hc_done", used), ("drv_done", used))
                    for k in range(2):
                        rows = bc_dram[par, k * NS + NG * g:k * NS + NG * g + NG, :]
                        sp.dma_start(bc_rep[:, g % 2, k, :, :], rows.unsqueeze(0).to_broadcast([128, NG, W])
                                     ).then_inc(s[f"bc_in{g % 2}"], 16)
                return f

            def h_load(e, _):
                waits(("hh_done", e), ("h_out", 16 * e + 16))
                sp.dma_start(h_res[:, :, :], h_dram[e]).then_inc(s["hres_in"], 16)

            def store(e, _):
                waits(("outb_done", e + 1))
                sp.dma_start(out[e], outb[:, :, :]).then_inc(s["out_stored"], 16)

            program({"K x": x_next, "K txt": txt_load, "F hstore": h_store, "F bcst": bc_store,
                     "F bc 0": bc_load(0), "F bc 1": bc_load(1), "C bc 2": bc_load(2), "C bc 3": bc_load(3),
                     "E hres": h_load, "E store": store}, sp)
            sp.wait_ge(s["out_stored"], 16 * NP)

        @block.gpsimd
        def _(pool):
            def drive(c):
                half, g, slot = c % H2, c // H2, c % 2

                def f(m, par):
                    n = NCH * m + c
                    if half == 0:
                        pool.wait_ge(s[f"bc_in{g % 2}"], 32 * (CH // 2 * m + g // 2 + 1))
                    if c == 0:
                        pool.wait_ge(s["dtu_done"], m + 1)
                    need(pool, "scan_done", n - 1)
                    pool.tensor_tensor(drv[:, slot, :, :], dtu[:, par, half:half + 1, :].to_broadcast([128, NG, W]),
                                       bc_rep[:, g % 2, 0, :, :], ALU.mult).then_inc(s["drv_done"], 1)
                return f

            def fold(c):
                slot = c % 2

                def f(m, _):
                    n = NCH * m + c
                    pool.wait_ge(s["hc_done"], n + 1)
                    x = hst[:, slot, :, :]
                    pool.tensor_tensor(x[:, 0:2], x[:, 0:2], x[:, 2:4], ALU.add).then_inc(s["hsum_done"], 1)
                    pool.wait_ge(s["hsum_done"], n + 1)
                    pool.tensor_tensor(x[:, 0], x[:, 0], x[:, 1], ALU.add).then_inc(s["hsum2_done"], 1)
                return f

            def select(e, _):
                pool.wait_ge(s["idx_done"], PAIR * e + PAIR)
                need(pool, "outb_part", PAIR * e)
                pool.tensor_tensor(top_seen[:, :, :], top8[:, :, :],
                                   ones_s[:, 0:PAIR * 8].rearrange("p (b e) -> p b e", b=PAIR), ALU.mult
                                   ).then_inc(s["top_read"], 1)
                for b in range(PAIR):
                    x = pool.value_load(idx8[0:1, b, 0:1], min_val=0, max_val=E - 1)
                    pool.dma_start(wsel[:, b, :], wexp[bass.ds(x, 1)].rearrange("a p n -> (a p) n")
                                   ).then_inc(s["wsel_in"], 16)

            pool.wait_ge(s["consts_in"], ALL_CONSTS)
            pool.wait_ge(s["preset_done"], PRESETS)
            program({f"C drv {c}": drive(c) for c in range(NCH)} | {f"C fold {c}": fold(c) for c in range(NCH)}
                    | {"E wsel": select}, pool)

        @block.scalar
        def _(act):
            A = act.activation
            LOGEXP, GELU = "natural_log_exp_and_others", "gelu_and_others"
            act.wait_ge(s["consts_in"], ALL_CONSTS)
            act.wait_ge(s["preset_done"], PRESETS)
            act.preload_act_table_set(LOGEXP)
            A(a_neg[:, :], col("a_log", 0, H2 * NS), ACT.Exp).then_inc(s["a_exp"], 1)
            A(ln_unit[:, :], zero_s[:, :], ACT.Ln, bias=unit_s[:, :]).then_inc(s["a_exp"], 1)
            act.wait_ge(s["a_done"], 1)
            act.wait_ge(s["scaled_done"], 4)

            def square(k, sq_t, cen_t):
                def f(r, _):
                    act.wait_ge(s[f"ln{k}_cen"], r + 1)
                    A(sq_t[:, :], cen_t[:, :], ACT.Square).then_inc(s[f"ln{k}_sq"], 1)
                return f

            def invert(k, rstd_t, var_ps, rsq=None, used=None):
                def f(r, par):
                    act.wait_ge(s[f"ln{k}_var"], r + 1)
                    A(rstd_t[:, :], var_ps, ACT.Ln, bias=eps_s[:, :]).then_inc(s[f"ln{k}_lnv"], 1)
                    act.wait_ge(s[f"ln{k}_lnv"], r + 1)
                    A(rstd_t[:, :], rstd_t[:, :], ACT.Exp, scale=-0.5).then_inc(s[f"ln{k}_rstd"], 1)
                    if rsq:
                        act.wait_ge(s[f"ln{k}_rstd"], r + 1)
                        need(act, used[0], used[1](r))
                        A(rsq(par), rstd_t[:, :], ACT.Square).then_inc(s[f"ln{k}_rsq"], 1)
                return f

            def u_evac(f, _):
                act.wait_ge(s["in_mm"], 2 * f + 1)
                need(act, "conv_step", H2 * TAPS * f)
                A(u_pad[:, :, TAPS - 1:], fe[:, :, 0:W].rearrange("p h (b t) -> p h b t", b=PAIR),
                  ACT.Copy).then_inc(s["u_evac"], 1)

            def z_tanh(f, _):
                act.wait_ge(s["in_mm"], 2 * f + 2)
                need(act, "dt_done", f)
                A(zt[:, :, :], fe[:, :, 0:W], ACT.Tanh, scale=0.5).then_inc(s["zt_done"], 1)

            def u_tanh(f, _):
                act.wait_ge(s["conv_step"], H2 * TAPS * (f + 1))
                A(th[:, :, :], cv[:, :, :], ACT.Tanh).then_inc(s["th_done"], 1)

            def xd_evac(f, _):
                act.wait_ge(s["xp_mm"], f + 1)
                need(act, "dt_mm", f)
                need(act, "bc_out", 16 * f)
                A(xd[0:RANK, :], fe[0:RANK, 1, 0:W], ACT.Copy).then_inc(s["xd_evac"], 1)
                A(xd[32:64, :], fe[32:64, 1, 0:W], ACT.Copy).then_inc(s["xd_evac"], 1)

            def sp_split(f, par):
                v = fe[:, :, 0:W]
                act.wait_ge(s["dt_mm"], f + 1)
                act.wait_ge(s["zs_done"], f + 1)
                A(sp_e[:, :, :], v, ACT.Abs).then_inc(s["sp_step"], 1)
                A(dt[:, par, :, :], v, ACT.Relu).then_inc(s["sp_step"], 1)

            def sp_exp(f, _):
                act.wait_ge(s["sp_step"], 5 * f + 1)
                A(sp_e[:, :, :], sp_e[:, :, :], ACT.Exp, scale=-1.0).then_inc(s["sp_step"], 1)

            def sp_log(f, _):
                act.wait_ge(s["sp_step"], 5 * f + 3)
                act.wait_ge(s["u_done"], f + 1)
                A(sp_l[:, :, :], sp_e[:, :, :], ACT.Relu, bias=neg_small[:, :]).then_inc(s["sp_step"], 1)
                act.wait_ge(s["sp_step"], 5 * f + 4)
                A(sp_l[:, :, :], sp_l[:, :, :], ACT.Ln, bias=unit_s[:, :], scale=1 / (1 + SMALL)).then_inc(s["sp_step"], 1)

            def decay(c):
                half, g, slot = c % H2, c // H2, c % 2

                def f(m, par):
                    if c == 0:
                        act.wait_ge(s["dt_done"], m + 1)
                    need(act, "scan_done", NCH * m + c - 1)
                    src = dt[:, par, half, :].rearrange("p (b t) -> p b t", b=PAIR)[:, :, 1:T]
                    for j in range(NG):
                        k = half * NS + g * NG + j
                        last = A(dec[:, slot, j, :, 1:T], src, ACT.Exp, scale=a_neg[:, k:k + 1])
                    last.then_inc(s["dec_done"], 1)
                return f

            def qk_evac(a, _):
                act.wait_ge(s["qk_mm"], a + 1)
                for g in range(GRP):
                    A(qT[:, g, :], ap[:, g, 0:W], ACT.Identity, bias=col("bq", g),
                      scale=HD ** -0.5).then_inc(s["qk_done"], 1)
                for g in range(GRP):
                    A(kT[:, g, :], ap[:, 2 + g, 0:W], ACT.Identity, bias=col("bk", g)).then_inc(s["qk_done"], 1)

            def v_evac(a, _):
                act.wait_ge(s["v_mm"], a + 1)
                for t, (_, n) in enumerate(KTILES):
                    last = A(v_s[0:n, :, t, :, 0:HD],
                             ap[0:n, 0, 0:512].rearrange("p (b t h e) -> p b t h e", b=PAIR, t=2, h=HEADS)[:, :, t],
                             ACT.Copy)
                last.then_inc(s["v_done"], 1)

            def probs(b, t):
                n = KTILES[t][1]

                def f(a, _):
                    need(act, "pv_mm", PAIR * a + b)
                    act.wait_ge(s["st_mm"], 4 * a + 2 * b + t + 1)
                    A(pT[0:n, t, :, :].rearrange("p (g e) q -> p g (e q)", g=4), ap[0:n, :, 0:W],
                      ACT.Exp).then_inc(s["p_done"], 1)
                return f

            def o_evac(b):
                def f(a, _):
                    act.wait_ge(s["pv_mm"], PAIR * a + b + 1)
                    need(act, "o_done", PAIR * a + b)
                    A(o_sb[:, :, :].rearrange(flat), ap[:, 0, 0:W], ACT.Copy).then_inc(s["oev_done"], 1)
                return f

            def inv_sum(b):
                def f(a, _):
                    act.wait_ge(s["sel_mm"], PAIR * a + b + 1)
                    r = rden[:, :, :].rearrange(flat)
                    A(r, ap[:, 1, 0:W], ACT.Ln).then_inc(s["rd_ln"], 1)
                    act.wait_ge(s["rd_ln"], PAIR * a + b + 1)
                    A(r, r, ACT.Exp, scale=-1.0).then_inc(s["rd_done"], 1)
                return f

            def gelu(first):
                def f(e, _):
                    need(act, "f2_mm", e)
                    for j in (first, first + 1):
                        act.wait_ge(s["f1_mm"], FC * e + j + 1)
                        A(hid[:, j, :], fe[:, j % 2, 0:W], ACT.Gelu, bias=col("b1", j)).then_inc(s["gelu_done"], 1)
                return f

            def expert(e, _):
                act.wait_ge(s["lgm_done"], PAIR * e + PAIR)
                A(lge[:, :, :], lgm[:, :, :], ACT.Exp).then_inc(s["lge_done"], 1)

            def tables(steps):
                own = [n for n in ORDER if n in ("F zt", "F th", "E ga", "E gb")]
                def loads(n):
                    step, mine = steps[n], [k for k in own if k[0] == n[0]]

                    def f(r, par):
                        i = r + LAG[n[0]]
                        alone = isinstance(i, int) and not LAG["E"] <= i < NP
                        here = mine if alone else own
                        if n == here[0]:
                            act.preload_act_table_set(GELU)
                        step(r, par)
                        if n == here[-1]:
                            act.preload_act_table_set(LOGEXP)
                    return f
                return steps | {n: loads(n) for n in own}

            program(tables(
                {"F sq": square(0, sq0, cen0), "F rstd": invert(0, rstd0, fe[:, 0, 0:W], lambda par: x0[:, par, :], ("r1_done", lambda f: f - 1)), "F u_ev": u_evac,
                 "F zt": z_tanh, "F th": u_tanh, "F xd": xd_evac, "F sp_v": sp_split, "F sp_e": sp_exp,
                 "F sp_l": sp_log,
                 "A sq": square(1, sq1, cen1), "A rstd": invert(1, rstd1, ap[:, 3, 0:W], lambda par: h1[:, par, :], ("r2_done", lambda a: a - 1)), "A qk_ev": qk_evac,
                 "A v_ev": v_evac,
                 "E2 sq": square(2, sq, cen), "E2 rstd": invert(2, rstd, fe[:, 1, 0:W]), "E ga": gelu(0),
                 "E gb": gelu(2),
                 "E3 sq": square(3, sq, cen), "E3 rstd": invert(3, rstd, fe[:, 0, 0:W]),
                 "E4 sq": square(4, sq, cen), "E4 rstd": invert(4, rstd, fe[:, 0, 0:W]), "E lge": expert}
                | {f"C dec {c}": decay(c) for c in range(NCH)}
                | {f"A pr{b}{t}": probs(b, t) for b in range(PAIR) for t in range(2)}
                | {f"{A_OR_B[b]} o_ev{b}": o_evac(b) for b in range(PAIR)}
                | {f"{A_OR_B[b]} rd{b}": inv_sum(b) for b in range(PAIR)}), act)

        @block.tensor
        def _(pe):
            def mm(out_ps, lhsT, rhs, first=True, last=True):
                return pe.matmul(out_ps, lhsT, rhs, start=first, stop=last)

            pe.wait_ge(s["consts_in"], ALL_CONSTS)
            pe.wait_ge(s["preset_done"], PRESETS)
            pe.wait_ge(s["scaled_done"], 4)
            for g in range(GRP):
                last = mm(ap[:, 0, 0:1], ow_s[:, g, :], col("bv", g), g == 0, g == GRP - 1)
            last.then_inc(s["bvo_mm"], 1)
            pe.wait_ge(s["prep_done"], 1)

            def tok(t, _):
                pe.wait_ge(s["x_in"], 16 * t + 16)
                need(pe, "sp_step", 5 * (t - 1) + 2)
                need(pe, "gb_done", t - 3)
                for k in range(KT):
                    last = mm(fe[:, 1, 0:PAIR * NPATCH], tokw_s[:, k, :], x_t[:, k, :], k == 0, k == KT - 1)
                last.then_inc(s["tok_mm"], 1)

            def mean(k, bank, src, *ready):
                def f(r, _):
                    for name, count in ready:
                        need(pe, name, count(r))
                    mm(bank, mean_w[:, :], src).then_inc(s[f"ln{k}_mean"], 1)
                return f

            def var(k, bank, sq_t):
                def f(r, _):
                    pe.wait_ge(s[f"ln{k}_sq"], r + 1)
                    mm(bank, mean_w[:, :], sq_t[:, :]).then_inc(s[f"ln{k}_var"], 1)
                return f

            def in_u(f, par):
                pe.wait_ge(s["ln0_out"], f + 1)
                need(pe, "ln2_lnv", f - 2)
                for j in range(2):
                    last = mm(fe[:, j, 0:W], inw_s[:, j, :], x0[:, par, :])
                last.then_inc(s["in_mm"], 1)

            def in_z(f, par):
                pe.wait_ge(s["u_evac"], f + 1)
                for j in range(2):
                    last = mm(fe[:, j, 0:W], inw_s[:, 2 + j, :], x0[:, par, :])
                last.then_inc(s["in_mm"], 1)

            def x_proj(f, par):
                pe.wait_ge(s["u_done"], f + 1)
                need(pe, "gelu_done", FC * (f - 2))
                for h in range(H2):
                    last = mm(fe[0:64, 1, 0:W], xw_s[:, h, :], u[:, par, h, :], h == 0, h == H2 - 1)
                last.then_inc(s["xp_mm"], 1)

            def dt_proj(f, _):
                pe.wait_ge(s["xd_evac"], 2 * f + 2)
                need(pe, "ln3_lnv", f - 2)
                for h in range(H2):
                    last = mm(fe[:, h, 0:W], dtw_s[:, h, :], xd[0:RANK + 1, :])
                last.then_inc(s["dt_mm"], 1)

            def state_sum(c):
                half, g, slot = c % H2, c // H2, c % 2

                def f(m, _):
                    pe.wait_ge(s["hsum2_done"], NCH * m + c + 1)
                    if c == 0:
                        need(pe, "r1_done", m)
                    mm(yp[:, half, 0:W], ident_s[:, :], hst[:, slot, 0, :], g == 0, g == CH - 1
                       ).then_inc(s["y_mm"], 1)
                return f

            def out_proj(m, _):
                pe.wait_ge(s["g_done"], m + 1)
                for h in range(H2):
                    last = mm(yp[:, 0, 0:W], outw_s[:, h, :], ypd[:, h, :], h == 0, h == H2 - 1)
                last.then_inc(s["op_mm"], 1)

            def qk(a, par):
                pe.wait_ge(s["ln1_out"], a + 1)
                need(pe, "r2_done", a)
                for g in range(2 * GRP):
                    last = mm(ap[:, g, 0:W], qkw_s[:, g, :], h1[:, par, :])
                last.then_inc(s["qk_mm"], 1)

            def values(a, par):
                pe.wait_ge(s["qk_done"], 4 * a + 1)
                for b in range(PAIR):
                    for t, (k0, n) in enumerate(KTILES):
                        o = (2 * b + t) * D
                        last = mm(ap[0:n, 0, o:o + D], h1[:, par, b * T + k0:b * T + k0 + n], vw_s[:, :])
                last.then_inc(s["v_mm"], 1)

            def scores(b, t):
                k0, n = KTILES[t]

                def f(a, _):
                    if t:
                        pe.wait_ge(s["max_done"], 4 * a + 2 * b + 1)
                    elif b:
                        pe.wait_ge(s["rd_ln"], PAIR * a + 1)
                    else:
                        pe.wait_ge(s["qk_done"], 4 * a + 4)
                        pe.wait_ge(s["v_done"], a + 1)
                    for e in range(GRP):
                        for g in range(4):
                            rows = slice(QUAD * g, QUAD * g + QUAD)
                            last = mm(ap[0:n, g, e * T:e * T + T], qT[rows, e, b * T + k0:b * T + k0 + n],
                                      kT[rows, e, b * T:b * T + T])
                    last.then_inc(s["s_mm"], 1)
                return f

            def turn(b):
                def f(a, _):
                    pe.wait_ge(s["max_done"], 4 * a + 2 * b + 2)
                    for e in range(GRP):
                        for t, (k0, n) in enumerate(KTILES):
                            last = pe.transpose(ap[:, 0, e * T + k0:e * T + k0 + n],
                                                negm[0:n, t, e, :, :].rearrange(flat), ident_s[0:n, 0:n])
                    last.then_inc(s["mt_mm"], 1)
                return f

            def scores_t(b, t):
                k0, n = KTILES[t]

                def f(a, _):
                    if t:
                        pe.wait_ge(s["p_done"], 4 * a + 2 * b + 1)
                    else:
                        pe.wait_ge(s["qaug_done"], PAIR * a + b + 1)
                    for e in range(GRP):
                        for g in range(4):
                            rows = slice(QUAD * g, QUAD * g + QUAD)
                            last = mm(ap[0:n, g, e * T:e * T + T], kT[rows, e, b * T + k0:b * T + k0 + n],
                                      qT[rows, e, b * T:b * T + T])
                    last.then_inc(s["st_mm"], 1)
                return f

            def pv(b):
                def f(a, _):
                    pe.wait_ge(s["p_done"], 4 * a + 2 * b + 2)
                    for e in range(GRP):
                        for t, (_, n) in enumerate(KTILES):
                            for g in range(4):
                                last = mm(ap[QUAD * g:QUAD * g + QUAD, 0, e * T:e * T + T],
                                          v_s[0:n, b, t, 4 * e + g, :], pT[0:n, t, GRP * g + e, :], t == 0, t == 1)
                    last.then_inc(s["pv_mm"], 1)
                return f

            def sums_to_rows(b):
                def f(a, _):
                    pe.wait_ge(s["oev_done"], PAIR * a + b + 1)
                    mm(ap[:, 1, 0:W], spread_s[:, :], o_sb[:, :, :].rearrange(flat)).then_inc(s["sel_mm"], 1)
                return f

            def attn_out(a, _):
                pe.wait_ge(s["o_done"], PAIR * a + PAIR)
                for g in range(GRP):
                    last = mm(ap[:, 0, 0:W], ow_s[:, g, :], oT[:, g, :, :].rearrange(flat), g == 0, g == GRP - 1)
                last.then_inc(s["ao_mm"], 1)

            def ffn1(first):
                def f(e, _):
                    if first:
                        pe.wait_ge(s["gelu_done"], FC * e + 2)
                    else:
                        pe.wait_ge(s["ln2_out"], e + 1)
                        need(pe, "zs_done", upto(e + 4))
                    for j in (first, first + 1):
                        mm(fe[:, j % 2, 0:W], w1_s[:, j, :], h2[:, :]).then_inc(s["f1_mm"], 1)
                return f

            def ffn2(e, _):
                pe.wait_ge(s["gelu_done"], FC * e + FC)
                for j in range(FC):
                    last = mm(fe[:, 0, 0:W], w2_s[:, j, :], hid[:, j, :], j == 0, j == FC - 1)
                last.then_inc(s["f2_mm"], 1)

            def logits(e, _):
                pe.wait_ge(s["msum_done"], e + 1)
                for b in range(PAIR):
                    last = mm(fe[0:1, 0, b * E:b * E + E], msum[:, b:b + 1], wg_s[:, :])
                last.then_inc(s["lg_mm"], 1)

            def gates(e, _):
                pe.wait_ge(s["gate_done"], e + 1)
                need(pe, "sp_step", 5 * (upto(e + 4) - 1) + 2)
                mm(fe[:, 1, 0:PAIR], ones_s[:, :], gate[:, :]).then_inc(s["gb_mm"], 1)

            def expert(e, _):
                pe.wait_ge(s["wsel_in"], 16 * PAIR * (e + 1))
                pe.wait_ge(s["gate_done"], e + 1)
                for b in range(PAIR):
                    last = mm(fe[:, 0, b * T:b * T + T], wsel[:, b, 0:D], xm[:, b, :])
                last.then_inc(s["y2_mm"], 1)

            program(
                {"K mm": tok,
                 "F mean": mean(0, fe[:, 0, 0:W], h_new[:, :, :].rearrange(flat), ("tok_done", lambda f: f + 1),
                                ("txt_in", lambda f: 16 * f + 16), ("outb_part", lambda f: PAIR * (f - 3))),
                 "F var": var(0, fe[:, 0, 0:W], sq0), "F in_u": in_u, "F in_z": in_z, "F xp": x_proj, "F dt": dt_proj,
                 "C out": out_proj,
                 "A mean": mean(1, ap[:, 3, 0:W], r1[:, :], ("r1_done", lambda a: a + 1), ("p_done", lambda a: 4 * a)),
                 "A var": var(1, ap[:, 3, 0:W], sq1), "A qk": qk, "A v": values, "B ao": attn_out,
                 "E2 mean": mean(2, fe[:, 1, 0:W], r2[:, :], ("r2_done", lambda e: e + 1),
                                 ("tok_done", lambda e: upto(e + 4))),
                 "E2 var": var(2, fe[:, 1, 0:W], sq), "E f1a": ffn1(0), "E f1b": ffn1(2), "E f2": ffn2,
                 "E3 mean": mean(3, fe[:, 0, 0:W], r3[:, :], ("r3_done", lambda e: e + 1)),
                 "E3 var": var(3, fe[:, 0, 0:W], sq),
                 "E4 mean": mean(4, fe[:, 0, 0:W], hh[:, :], ("hh_done", lambda e: e + 1),
                                 ("sp_step", lambda e: 5 * (upto(e + 4) - 1) + 2)),
                 "E4 var": var(4, fe[:, 0, 0:W], sq), "E lg": logits, "E gbm": gates, "E y2": expert}
                | {f"C sum {c}": state_sum(c) for c in range(NCH)}
                | {f"A s{b}{t}": scores(b, t) for b in range(PAIR) for t in range(2)}
                | {f"A st{b}{t}": scores_t(b, t) for b in range(PAIR) for t in range(2)}
                | {f"A mt{b}": turn(b) for b in range(PAIR)} | {f"A pv{b}": pv(b) for b in range(PAIR)}
                | {f"{A_OR_B[b]} sel{b}": sums_to_rows(b) for b in range(PAIR)}, pe)

        @block.vector
        def _(dve):
            V = dve

            def stt(out_, in0, scalar, in1, op0, op1):
                return V.scalar_tensor_tensor(out=out_, in0=in0, scalar=scalar, in1=in1, op0=op0, op1=op1)

            for t_, val in ((mean_w[:, :], 1.0 / D), (ones_s[:, :], 1.0), (eps_s[:, :], EPS),
                            (zero_s[:, :], 0.0), (neg_small[:, :], -SMALL), (unit_s[:, :], 1.0),
                            (u_pad[:, :, 0:TAPS - 1], 0.0), (dec[:, :, :, :, 0:1], 0.0), (xd[0:32, :], 1.0),
                            (v_s[:, :, :, :, HD:QUAD], 1.0), (negm[:, :, :, :, :], 0.0)):
                V.memset(t_, val).then_inc(s["preset_done"], 1)
            V.wait_ge(s["consts_in"], ALL_CONSTS)
            for b in range(PAIR):
                last = V.tensor_tensor(h_new[:, b, 0:1], col("cls"), col("pos"), ALU.mult)
            last.then_inc(s["preset_done"], 1)
            c0 = COLS["conv_w"][0]
            cw = colt[:, c0:c0 + H2 * TAPS + H2]
            V.tensor_scalar(cw, cw, 0.5, None, ALU.mult).then_inc(s["scaled_done"], 1)
            V.tensor_scalar(outw_s[:, :, :], outw_s[:, :, :], 0.5, None, ALU.mult).then_inc(s["scaled_done"], 1)
            bq = col("bq", 0, GRP)
            V.tensor_scalar(bq, bq, HD ** -0.5, None, ALU.mult).then_inc(s["scaled_done"], 1)
            V.tensor_scalar(col("g1"), col("g1"), -0.5, None, ALU.mult).then_inc(s["scaled_done"], 1)
            V.wait_ge(s["a_exp"], 2)
            V.tensor_scalar(a_neg[:, :], a_neg[:, :], -1.0, None, ALU.mult).then_inc(s["a_done"], 1)
            V.wait_ge(s["bvo_mm"], 1)
            V.tensor_tensor(bo_all[:, :], ap[:, 0, 0:1], col("bo"), ALU.add).then_inc(s["prep_done"], 1)
            V.wait_ge(s["scaled_done"], 4)
            V.wait_ge(s["preset_done"], PRESETS)
            V.wait_ge(s["prep_done"], 1)

            def pos(t, _):
                V.wait_ge(s["tok_mm"], t + 1)
                need(V, "h_out", 16 * t)
                p = col("pos", 1, NPATCH).unsqueeze(1).to_broadcast([128, PAIR, NPATCH])
                stt(h_new[:, :, 1:NIMG], fe[:, 1, 0:PAIR * NPATCH].rearrange("p (b n) -> p b n", b=PAIR),
                    col("tok_b"), p, ALU.add, ALU.mult).then_inc(s["tok_done"], 1)

            def center(k, src, mean_ps, cen_t):
                def f(r, _):
                    V.wait_ge(s[f"ln{k}_mean"], r + 1)
                    V.tensor_tensor(cen_t[:, :], src, mean_ps, ALU.subtract).then_inc(s[f"ln{k}_cen"], 1)
                return f

            def scale(k, cen_t, rstd_t, dst):
                def f(r, _):
                    V.wait_ge(s[f"ln{k}_rstd"], r + 1)
                    stt(cen_t[:, :], cen_t[:, :], col(f"g{k}"), rstd_t[:, :], ALU.mult, ALU.mult
                        ).then_inc(s[f"ln{k}_nrm"], 1)
                    V.wait_ge(s[f"ln{k}_nrm"], r + 1)
                    V.tensor_scalar(dst, cen_t[:, :], col(f"e{k}"), None, ALU.add).then_inc(s[f"ln{k}_out"], 1)
                return f

            def newton(k, r, rsq, var_ps, nrm, dst):
                V.wait_ge(s[f"ln{k}_rsq"], r + 1)
                stt(rsq, var_ps, eps_s[:, :], rsq, ALU.add, ALU.mult).then_inc(s[f"ln{k}_res"], 1)
                V.wait_ge(s[f"ln{k}_nrm"], r + 1)
                V.wait_ge(s[f"ln{k}_res"], r + 1)
                return stt(dst, rsq, 3.0, nrm, ALU.subtract, ALU.mult)

            def x0_out(f, par):
                V.wait_ge(s["ln0_rstd"], f + 1)
                stt(cen0[:, :], cen0[:, :], -0.5, rstd0[:, :], ALU.mult, ALU.mult).then_inc(s["ln0_nrm"], 1)
                newton(0, f, x0[:, par, :], fe[:, 0, 0:W], cen0[:, :], x0[:, par, :]).then_inc(s["ln0_out"], 1)

            def conv(f, _):
                V.wait_ge(s["u_evac"], f + 1)
                for k in range(TAPS):
                    for h in range(H2):
                        w = col("conv_w", h * TAPS + k)
                        src = u_pad[:, PAIR * h:PAIR * h + PAIR, k:k + T]
                        dst = cv[:, h, :].rearrange("p (b t) -> p b t", b=PAIR)
                        if k == 0:
                            V.tensor_scalar(dst, src, w, col("conv_b", h), ALU.mult,
                                            ALU.add).then_inc(s["conv_step"], 1)
                        else:
                            V.wait_ge(s["conv_step"], H2 * TAPS * f + H2 * (k - 1) + h + 1)
                            stt(dst, src, w, dst, ALU.mult, ALU.add).then_inc(s["conv_step"], 1)

            def z_silu(f, par):
                V.wait_ge(s["zt_done"], f + 1)
                stt(zs[:, par, :, :], zt[:, :, :], 1.0, fe[:, :, 0:W], ALU.add, ALU.mult).then_inc(s["zs_done"], 1)

            def u_silu(f, par):
                V.wait_ge(s["th_done"], f + 1)
                stt(u[:, par, :, :], th[:, :, :], 1.0, cv[:, :, :], ALU.add, ALU.mult).then_inc(s["u_done"], 1)

            def series(f, par):
                V.wait_ge(s["sp_step"], 5 * f + 3)
                need(V, "drv_done", NCH * (f - 1))
                c, p = sp_c[:, :, :], dtu[:, par, :, :]
                V.tensor_scalar(c, sp_e[:, :, :], SMALL, None, ALU.min).then_inc(s["lp_step"], 1)
                V.wait_ge(s["lp_step"], 6 * f + 1)
                V.tensor_scalar(p, c, -1 / 4, 1 / 3, ALU.mult, ALU.add).then_inc(s["lp_step"], 1)
                V.wait_ge(s["lp_step"], 6 * f + 2)
                V.tensor_tensor(p, p, c, ALU.mult).then_inc(s["lp_step"], 1)
                V.wait_ge(s["lp_step"], 6 * f + 3)
                stt(p, p, -1 / 2, c, ALU.add, ALU.mult).then_inc(s["lp_step"], 1)
                V.wait_ge(s["lp_step"], 6 * f + 4)
                stt(p, p, 1.0, c, ALU.add, ALU.mult).then_inc(s["lp_step"], 1)

            def dt_u(f, par):
                d, p = dt[:, par, :, :], dtu[:, par, :, :]
                V.wait_ge(s["lp_step"], 6 * f + 5)
                V.wait_ge(s["sp_step"], 5 * f + 5)
                stt(p, sp_l[:, :, :], ln_unit[:, :], p, ALU.subtract, ALU.add).then_inc(s["lp_step"], 1)
                V.wait_ge(s["lp_step"], 6 * f + 6)
                V.tensor_tensor(d, d, p, ALU.add).then_inc(s["dt_done"], 1)
                V.wait_ge(s["dt_done"], f + 1)
                V.tensor_tensor(p, d, u[:, par, :, :], ALU.mult).then_inc(s["dtu_done"], 1)

            def scan(c):
                slot = c % 2

                def f(m, _):
                    n = NCH * m + c
                    V.wait_ge(s["dec_done"], n + 1)
                    V.wait_ge(s["drv_done"], n + 1)
                    need(V, "y_mm", n - 1)
                    V.tensor_tensor_scan(hst[:, slot, :, :].rearrange(flat),
                                         dec[:, slot, :, :, :].rearrange("p j b t -> p (j b t)"),
                                         drv[:, slot, :, :].rearrange(flat), 0.0, ALU.mult,
                                         ALU.add).then_inc(s["scan_done"], 1)
                return f

            def times_c(c):
                g, slot = c // H2, c % 2

                def f(m, _):
                    V.wait_ge(s["scan_done"], NCH * m + c + 1)
                    x = hst[:, slot, :, :]
                    V.tensor_tensor(x, x, bc_rep[:, g % 2, 1, :, :], ALU.mult).then_inc(s["hc_done"], 1)
                return f

            def skip(h):
                def f(m, par):
                    V.wait_ge(s["y_mm"], NCH * m + NCH - 1 + h)
                    stt(ypd[:, h, :], u[:, par, h, :], col("dp", h), yp[:, h, 0:W], ALU.mult,
                        ALU.add).then_inc(s["ypd_done"], 1)
                return f

            def gated(m, par):
                V.wait_ge(s["ypd_done"], H2 * m + H2)
                V.tensor_tensor(ypd[:, :, :], ypd[:, :, :], zs[:, par, :, :], ALU.mult).then_inc(s["g_done"], 1)

            def r1_out(m, par):
                V.wait_ge(s["op_mm"], m + 1)
                V.tensor_tensor(r1[:, :], yp[:, 0, 0:W], x0[:, par, :], ALU.add).then_inc(s["r1_done"], 1)

            def h1_out(a, par):
                V.wait_ge(s["ln1_rstd"], a + 1)
                stt(cen1[:, :], cen1[:, :], col("g1"), rstd1[:, :], ALU.mult, ALU.mult).then_inc(s["ln1_nrm"], 1)
                newton(1, a, h1[:, par, :], ap[:, 3, 0:W], cen1[:, :], cen1[:, :]).then_inc(s["h1_scaled"], 1)
                V.wait_ge(s["h1_scaled"], a + 1)
                V.tensor_scalar(h1[:, par, :], cen1[:, :], col("e1"), None, ALU.add).then_inc(s["ln1_out"], 1)

            def maxima(b, t):
                n = KTILES[t][1]

                def f(a, _):
                    V.wait_ge(s["s_mm"], 4 * a + 2 * b + t + 1)
                    V.tensor_reduce(negm[0:n, t, :, :, HD].rearrange("p e g -> p g e"),
                                    ap[0:n, :, 0:W].rearrange("p g (e k) -> p g e k", e=GRP),
                                    AX.X, ALU.max, negate=True).then_inc(s["max_done"], 1)
                return f

            def q_augment(b):
                def f(a, _):
                    V.wait_ge(s["mt_mm"], PAIR * a + b + 1)
                    q = qT[:, :, b * T:b * T + T]
                    V.tensor_tensor(q, q, ap[:, 0, 0:W].rearrange("p (e k) -> p e k", e=GRP),
                                    ALU.add).then_inc(s["qaug_done"], 1)
                return f

            def o_out(b):
                def f(a, _):
                    V.wait_ge(s["rd_done"], PAIR * a + b + 1)
                    V.tensor_tensor(oT[:, :, b, :], o_sb[:, :, :], rden[:, :, :], ALU.mult).then_inc(s["o_done"], 1)
                return f

            def r2_out(a, par):
                V.wait_ge(s["ao_mm"], a + 1)
                stt(r2[:, :], ap[:, 0, 0:W], bo_all[:, :], h1[:, par, :], ALU.add, ALU.add).then_inc(s["r2_done"], 1)

            def r3_out(e, _):
                V.wait_ge(s["f2_mm"], e + 1)
                stt(r3[:, :], fe[:, 0, 0:W], col("b2"), h2[:, :], ALU.add, ALU.add).then_inc(s["r3_done"], 1)

            def add_res(e, _):
                V.wait_ge(s["ln3_out"], e + 1)
                V.wait_ge(s["hres_in"], 16 * e + 16)
                V.tensor_tensor(hh[:, :], hh[:, :], h_res[:, :, :].rearrange(flat), ALU.add).then_inc(s["hh_done"], 1)

            def xm_out(e, _):
                V.wait_ge(s["ln4_rstd"], e + 1)
                V.tensor_tensor(xm[:, :, :].rearrange(flat), cen[:, :], rstd[:, :], ALU.mult).then_inc(s["ln4_out"], 1)

            def pool_tokens(e, _):
                V.wait_ge(s["ln4_out"], e + 1)
                V.tensor_reduce(msum[:, :], xm[:, :, :], AX.X, ALU.add).then_inc(s["msum_done"], 1)

            def top(e, _):
                V.wait_ge(s["lg_mm"], e + 1)
                stt(lg[:, :, :], fe[0:1, 0, 0:PAIR * E].rearrange("p (b e) -> p b e", b=PAIR), 1.0 / T, bg_s[:, :, :],
                    ALU.mult, ALU.add).then_inc(s["lg_done"], 1)
                V.wait_ge(s["lg_done"], e + 1)
                need(V, "wsel_in", 16 * PAIR * e)
                need(V, "top_read", e)
                V.tensor_copy(lg_seen[:, :, :], lg[:, :, :])
                for b in range(PAIR):
                    V.max(top8[:, b, :], lg[:, b, :]).then_inc(s["top_done"], 1)
                for b in range(PAIR):
                    V.wait_ge(s["top_done"], PAIR * e + b + 1)
                    V.tensor_scalar(lgm[:, b, :], lg[:, b, :], top8[:, b, 0:1], None,
                                    ALU.subtract).then_inc(s["lgm_done"], 1)
                    V.max_index(idx8[:, b, :], top8[:, b, :], lg[:, b, :]).then_inc(s["idx_done"], 1)

            def gate_out(e, _):
                V.wait_ge(s["lge_done"], e + 1)
                V.tensor_reduce(den2[:, :], lge[:, :, :], AX.X, ALU.add).then_inc(s["den_done"], 1)
                V.wait_ge(s["den_done"], e + 1)
                V.reciprocal(gate[:, :], den2[:, :]).then_inc(s["gate_done"], 1)

            def gate_copy(e, _):
                V.wait_ge(s["gb_mm"], e + 1)
                V.tensor_copy(gate_b[:, :], fe[:, 1, 0:PAIR]).then_inc(s["gb_done"], 1)

            def final(e, _):
                V.wait_ge(s["gb_done"], e + 1)
                V.wait_ge(s["y2_mm"], e + 1)
                need(V, "out_stored", 16 * e)
                for b in range(PAIR):
                    V.tensor_scalar(outb[:, b, :], fe[:, 0, b * T:b * T + T], wsel[:, b, D:D + 1],
                                    gate_b[:, b:b + 1], ALU.add, ALU.mult).then_inc(s["outb_part"], 1)
                V.wait_ge(s["outb_part"], PAIR * e + PAIR)
                o = outb[:, :, :].rearrange(flat)
                V.tensor_tensor(o, o, hh[:, :], ALU.add).then_inc(s["outb_done"], 1)

            program(
                {"K pos": pos,
                 "F cen": center(0, h_new[:, :, :].rearrange(flat), fe[:, 0, 0:W], cen0), "F x0": x0_out,
                 "F conv": conv, "F zs": z_silu, "F u": u_silu, "F poly": series, "F dtu": dt_u,
                 "C y0": skip(0), "C y1": skip(1), "C g": gated, "C r1": r1_out,
                 "A cen": center(1, r1[:, :], ap[:, 3, 0:W], cen1), "A nrm": h1_out,
                 "B r2": r2_out,
                 "E2 cen": center(2, r2[:, :], fe[:, 1, 0:W], cen), "E2 nrm": scale(2, cen, rstd, h2[:, :]),
                 "E r3": r3_out,
                 "E3 cen": center(3, r3[:, :], fe[:, 0, 0:W], cen), "E3 nrm": scale(3, cen, rstd, hh[:, :]),
                 "E hh": add_res,
                 "E4 cen": center(4, hh[:, :], fe[:, 0, 0:W], cen), "E4 xm": xm_out, "E msum": pool_tokens,
                 "E top": top, "E gate": gate_out, "E gbc": gate_copy, "E out": final}
                | {f"C scan {c}": scan(c) for c in range(NCH)} | {f"C hc {c}": times_c(c) for c in range(NCH)}
                | {f"A max{b}{t}": maxima(b, t) for b in range(PAIR) for t in range(2)}
                | {f"A qaug{b}": q_augment(b) for b in range(PAIR)} | {f"{A_OR_B[b]} o{b}": o_out(b) for b in range(PAIR)}, dve)


def _layout(a):
    f = np.float32

    def heads(x):
        o = np.zeros((GRP, 4, QUAD) + x.shape[1:], f)
        o[:, :, :HD] = x.reshape((GRP, 4, HD) + x.shape[1:])
        return o.reshape((GRP, 4 * QUAD) + x.shape[1:])

    x = a["x"].reshape(NP, PAIR, C_IN, GRID, PATCH, GRID, PATCH).transpose(0, 2, 4, 6, 1, 3, 5)
    lay = {"xh": x.reshape(NP, KP, KT, PAIR * NPATCH)}
    lay["txt"] = a["txt"].reshape(NP, PAIR, NTXT, D).transpose(0, 3, 1, 2)
    lay["tokw"] = a["L0_tok_W"].T.reshape(KP, KT, D)
    inw = a["L0_attn_in_proj_w"].T.reshape(D, 4, 128)
    lay["inw"] = inw
    xp = a["L0_attn_x_proj_w"]
    xw = np.zeros((64, DI), f)
    xw[0:RANK], xw[32:64] = xp[0:RANK], xp[RANK:]
    lay["xw"] = xw.T.reshape(H2, 128, 64).transpose(1, 0, 2)
    dtw = np.concatenate([a["L0_attn_dt_proj_w"].T, a["L0_attn_dt_proj_b"][None]], 0)
    lay["dtw"] = dtw.reshape(RANK + 1, H2, 128)
    lay["outw"] = a["L0_attn_out_proj_w"].T.reshape(H2, 128, D).transpose(1, 0, 2)
    qw, kw, vw = a["L0_attn_mha_in_w"].reshape(3, D, D)
    qb, kb, vb = a["L0_attn_mha_in_b"].reshape(3, D)
    lay["qkw"] = np.concatenate([heads(qw), heads(kw)], 0).transpose(2, 0, 1)
    lay["vw"] = vw.T
    lay["ow"] = heads(a["L0_attn_mha_out_w"].T).transpose(1, 0, 2)
    lay["w1"] = a["L0_attn_w1"].T.reshape(D, FC, 128)
    lay["w2"] = a["L0_attn_w2"].T.reshape(FC, 128, D).transpose(1, 0, 2)
    lay["wg"] = a["L0_ffn_Wg"]
    lay["bgrow"] = np.stack([a["L0_ffn_bg"]] * PAIR)[None]
    wexp = np.concatenate([a["L0_ffn_We"].transpose(1, 0, 2), a["L0_ffn_be"].T[:, :, None]], 2)
    lay["wexp"] = wexp.transpose(1, 0, 2)
    lay["ident"] = np.eye(128, dtype=f)
    spread = np.zeros((4, QUAD, 4, QUAD), f)
    for g in range(4):
        spread[g, HD, g] = 1.0
    lay["spread"] = spread.reshape(128, 128)

    def half(v):
        return v.reshape(H2, 128, -1).transpose(1, 0, 2).reshape(128, -1)

    bk = heads(kb).reshape(GRP, 4, QUAD)
    bk[:, :, HD] = 1.0
    parts = {
        "tok_b": a["L0_tok_b"], "cls": a["L0_tok_class_token"][0], "pos": a["L0_tok_pos_embed"].T,
        "conv_w": half(a["L0_attn_conv_w"]), "conv_b": half(a["L0_attn_conv_b"]), "a_log": half(a["L0_attn_A_log"]),
        "dp": half(a["L0_attn_Dp"]), "bq": heads(qb).T, "bk": bk.reshape(GRP, 128).T, "bv": heads(vb).T,
        "bo": a["L0_attn_mha_out_b"], "g1": a["L0_attn_ln1_g"], "e1": a["L0_attn_ln1_b"], "g2": a["L0_attn_ln2_g"],
        "e2": a["L0_attn_ln2_b"], "g3": a["L0_attn_ln3_g"], "e3": a["L0_attn_ln3_b"],
        "b1": a["L0_attn_b1"].reshape(FC, 128).T, "b2": a["L0_attn_b2"]}
    lay["cols"] = np.concatenate([parts[n].reshape(128, w) for n, (_, w) in COLS.items()], 1)
    return lay


_ORDER = ["xh", "txt", "cols", "tokw", "inw", "xw", "dtw", "outw", "qkw", "vw", "ow", "w1", "w2", "wg", "bgrow",
          "wexp", "ident", "spread"]


def kernel(**inputs):
    import concourse.bacc as _bacc
    from concourse.bass_utils import run_bass_kernel_spmd as _run

    lay = _layout({k: np.asarray(v) for k, v in inputs.items()})
    nc = _bacc.Bacc("TRN2", target_bir_lowering=False, num_devices=1)
    arrays, args = {}, []
    for name in _ORDER:
        arr = np.ascontiguousarray(lay[name])
        arrays[f"in_{name}"] = arr
        args.append(nc.dram_tensor(f"in_{name}", arr.shape, mybir.dt.from_np(arr.dtype), kind="ExternalInput").ap())
    args.append(nc.dram_tensor("out_0", (NP, D, PAIR, T), F32, kind="ExternalOutput").ap())
    fusion_kernel(nc, *args)
    r = _run(nc, [arrays], core_ids=[0])
    got = r.results[0]["out_0"]
    return np.ascontiguousarray(got.transpose(0, 2, 3, 1).reshape(B, T, D))
```

```python
from contextlib import ExitStack

import numpy as np

import concourse.bass as bass
from concourse import mybir

F32 = mybir.dt.float32
U32 = mybir.dt.uint32
ALU = mybir.AluOpType
ACT = mybir.ActivationFunctionType
AX = mybir.AxisListType

B, C_IN, IMG, PATCH = 64, 3, 224, 28
GRID = IMG // PATCH
NPATCH = GRID * GRID
NIMG = NPATCH + 1
NTXT = 128
T = NIMG + NTXT
D = 128
DI = 256
H2 = DI // 128
NS = 16
TAPS = 4
RANK = 8
HEADS, HD = 8, 16
QUAD = 32
GRP = HEADS // 4
FF = 4 * D
FC = FF // 128
E = 16
PAIR = 2
NP = B // PAIR
W = PAIR * T
IN_D = C_IN * PATCH * PATCH
KP = 112
KT = IN_D // KP
NG = 4
CH = NS // NG
NCH = H2 * CH
KTILES = ((0, 128), (128, T - 128))
EPS = 1e-5
SMALL = 1 / 64
LN_2, LN_3 = -0.49997422, 0.32797226

COLS = {}
for _n, _w in (("tok_b", 1), ("cls", 1), ("pos", NIMG), ("conv_w", H2 * TAPS), ("conv_b", H2), ("a_log", H2 * NS),
               ("dp", H2), ("bq", GRP), ("bk", GRP), ("bv", GRP), ("bo", 1), ("g1", 1), ("e1", 1), ("g2", 1),
               ("e2", 1), ("g3", 1), ("e3", 1), ("b1", FC), ("b2", 1)):
    COLS[_n] = (sum(w for _, w in COLS.values()), _w)
NCOL = sum(w for _, w in COLS.values())

ORDER = (
    "C dec 0", "C drv 0", "C scan 0", "B o_ev1", "B sel1", "F mean", "C dec 1", "B rd1", "A mean", "F cen",
    "C drv 1", "E hres", "C drv 2", "B o1", "A sq", "A var", "F sq", "C scan 1", "B ao", "C dec 2", "B r2",
    "E2 mean", "C hc 0", "E2 cen", "A rstd", "E2 sq", "A nrm", "C fold 0", "F var", "E2 var", "C hc 1", "A qk",
    "F rstd", "C dec 3", "E2 rstd", "C bc 2", "C sum 0", "A qk_ev", "C fold 1", "F x0", "F in_u", "C scan 2",
    "C sum 1", "C hc 2", "F u_ev", "A v", "F in_z", "A v_ev", "E2 nrm", "C fold 2", "F zt", "F zs", "F tap",
    "A s00", "F cv1", "E f1a", "C drv 3", "F cv2", "E ga", "C drv 4", "A max00", "F cv3", "E f1b", "A s01", "E gb",
    "E f2", "C scan 3", "A max01", "F th", "F u", "A mt0", "E r3", "C dec 4", "C sum 2", "A qaug0", "E3 mean",
    "C dec 5", "A st00", "F xp", "E3 cen", "C hc 3", "E3 sq", "C drv 5", "C scan 4", "A pr00", "F xd", "E3 var",
    "E3 rstd", "C bc 3", "C fold 3", "C hc 4", "A st01", "E3 nrm", "F dt", "A pr01", "C fold 4", "C sum 3",
    "F sp_v", "C drv 6", "F sp_e", "F bcst", "E hh", "A pv0", "E4 mean", "F hstore", "A o_ev0", "C scan 5",
    "E4 cen", "C hc 5", "E4 sq", "A sel0", "E4 var", "F poly0", "A rd0", "E4 rstd", "E4 xm", "A s10", "E msum",
    "E lg", "C dec 6", "C fold 5", "C sum 4", "A max10", "C drv 7", "C sum 5", "E top", "A s11", "C dec 7",
    "E lge", "C scan 6", "E gate", "F sp_l", "E gbm", "E gbc", "K mm0", "A max11", "A mt1", "E wsel", "C hc 6",
    "F poly1", "A qaug1", "C fold 6", "F poly2", "K mm1", "A st10", "C scan 7", "A o0", "E y2", "E gbias",
    "C hc 7", "A pr10", "F dtl", "K mm2", "A st11", "K pos", "F dts", "C sum 6", "F dtu", "E outa", "C fold 7",
    "F bc 0", "E out", "C sum 7", "C y0", "K x", "C y1", "K txt", "A pr11", "A pv1", "F bc 1", "C g", "E store",
    "C out", "C r1",
)
LAG = {"K": -1, "F": 0, "C": 1, "A": 2, "B": 3, "E": 3}
A_OR_B = "AB"


def fusion_kernel(nc, xh, txt, cols, tokw, inw, xw, dtw, outw, qkw, vw, ow, w1, w2, wg, bgrow, wexp, ident, spread,
                  out):
    bc_dram = nc.dram_tensor("bc_scratch", [2, 2 * NS, W], F32, kind="Internal").ap()
    h_dram = nc.dram_tensor("h_scratch", [NP, D, PAIR, T], F32, kind="Internal").ap()
    with ExitStack() as ctx:
        def sb(name, shape, dt=F32):
            return ctx.enter_context(nc.sbuf_tensor(name, shape, dt))

        def sem(name):
            return ctx.enter_context(nc.semaphore(name))

        colt = sb("colt", [128, NCOL])
        tokw_s = sb("tokw_s", [KP, KT, D])
        inw_s = sb("inw_s", [128, 4, 128])
        xw_s = sb("xw_s", [128, H2, 64])
        dtw_s = sb("dtw_s", [RANK + 1, H2, 128])
        outw_s = sb("outw_s", [128, H2, 128])
        qkw_s = sb("qkw_s", [128, 2 * GRP, 128])
        vw_s = sb("vw_s", [128, D])
        ow_s = sb("ow_s", [128, GRP, D])
        w1_s = sb("w1_s", [128, FC, 128])
        w2_s = sb("w2_s", [128, FC, D])
        wg_s = sb("wg_s", [128, E])
        bg_s = sb("bg_s", [1, PAIR, E])
        ident_s = sb("ident_s", [128, 128])
        spread_s = sb("spread_s", [128, 128])
        mean_w = sb("mean_w", [128, 128])
        center_w = sb("center_w", [128, 128])
        ones_s = sb("ones_s", [1, 128])
        eps_s = sb("eps_s", [128, 1])
        zero_s = sb("zero_s", [128, 1])
        neg_small = sb("neg_small", [128, 1])
        unit_s = sb("unit_s", [128, 1])
        ln_unit = sb("ln_unit", [128, 1])
        a_neg = sb("a_neg", [128, H2 * NS])
        bo_all = sb("bo_all", [128, 1])

        def col(name, i=0, n=1):
            o = COLS[name][0] + i
            return colt[:, o:o + n]

        x_t = sb("x_t", [KP, KT, PAIR * NPATCH])
        h_new = sb("h_new", [128, PAIR, T])
        cen0 = sb("cen0", [128, W])
        sq0 = sb("sq0", [128, W])
        rstd0 = sq0
        x0 = sb("x0", [128, 2, W])
        u_pad = sb("u_pad", [128, H2 * PAIR, T + TAPS - 1])
        cv = sb("cv", [128, H2, W])
        th = sb("th", [128, H2, W])
        zt = sb("zt", [128, H2, W])
        sp_c, sp_l, sp_e = cv, th, zt
        xd = sb("xd", [64, W])
        u = sb("u", [128, 2, H2, W])
        zs = sb("zs", [128, 2, H2, W])
        dt = sb("dt", [128, 2, H2, W])
        dtu = sb("dtu", [128, 2, H2, W])
        bc_rep = sb("bc_rep", [128, 2, 2, NG, W])
        dec = sb("dec", [128, 2, NG, PAIR, T])
        drv = sb("drv", [128, 2, NG, W])
        hst = sb("hst", [128, 2, NG, W])
        ypd = sb("ypd", [128, H2, W])
        r1 = sb("r1", [128, W])
        cen1 = sb("cen1", [128, W])
        sq1 = sb("sq1", [128, W])
        rstd1 = sq1
        h1 = sb("h1", [128, 2, W])
        qT = sb("qT", [128, GRP, W])
        kT = sb("kT", [128, GRP, W])
        v_s = sb("v_s", [128, PAIR, 2, HEADS, QUAD])
        negm = sb("negm", [128, 2, GRP, 4, QUAD])
        pT = sb("pT", [128, 2, HEADS, T])
        o_sb = sb("o_sb", [128, GRP, T])
        rden = sb("rden", [128, GRP, T])
        oT = sb("oT", [128, GRP, PAIR, T])
        r2 = sb("r2", [128, W])
        cen = sb("cen", [128, W])
        sq = sb("sq", [128, W])
        rstd = sq
        h_res = sb("h_res", [128, PAIR, T])
        h2 = sb("h2", [128, W])
        hid = sb("hid", [128, FC, W])
        r3 = sb("r3", [128, W])
        hh = sb("hh", [128, W])
        xm = sb("xm", [128, PAIR, T])
        msum = sb("msum", [128, PAIR])
        lg = sb("lg", [1, PAIR, E])
        top8 = sb("top8", [1, PAIR, 8])
        idx8 = sb("idx8", [1, PAIR, 8], U32)
        top_seen = sb("top_seen", [1, PAIR, 8])
        lg_seen = sb("lg_seen", [1, PAIR, E])
        lgm = sb("lgm", [1, PAIR, E])
        lge = sb("lge", [1, PAIR, E])
        den2 = sb("den2", [1, PAIR])
        gate = sb("gate", [1, PAIR])
        gate_b = sb("gate_b", [128, PAIR])
        gated_b = sb("gated_b", [128, PAIR])
        wsel = sb("wsel", [128, PAIR, D + 1])
        outb = sb("outb", [128, PAIR, T])

        fe = ctx.enter_context(nc.psum_tensor("fe", [128, 2, 512], F32))
        yp = ctx.enter_context(nc.psum_tensor("yp", [128, H2, 512], F32))
        ap = ctx.enter_context(nc.psum_tensor("ap", [128, 4, 512], F32))

        s = {n: sem(n) for n in (
            "consts_in", "preset_done", "a_exp", "a_done", "scaled_done", "bvo_mm", "prep_done",
            "x_in", "txt_in", "tok_mm", "tok_done", "h_out",
            "in_mm", "u_evac", "zt_done", "zs_done", "tap_done", "conv_step", "th_done", "u_done",
            "xp_mm", "xd_evac", "bc_out", "b_in0", "b_in1", "c_in0", "c_in1", "dt_mm", "sp_step", "lp_step",
            "dt_done", "dtu_done",
            "dec_done", "drv_done", "scan_done", "hc_done", "hsum_done", "hsum2_done", "y_mm", "ypd_done", "g_done",
            "op_mm", "r1_done",
            "h1_scaled", "qk_mm", "qk_done", "v_mm", "v_done", "s_mm", "max_done", "mt_mm", "qaug_done",
            "st_mm", "p_done", "pv_mm", "oev_done", "sel_mm", "rd_ln", "rd_done", "o0_done", "o1_done",
            "ao_mm", "r2_done",
            "f1_mm", "gelu_done", "f2_mm", "r3_done", "hres_in", "hh_done", "msum_done", "lg_mm", "lg_done",
            "top_done", "idx_done", "top_read", "lgm_done", "lge_done", "den_done", "gate_done", "gb_mm", "gb_done",
            "wsel_in", "gbias_done", "y2_mm", "outb_part", "outb_done", "out_stored")}
        for k in range(5):
            for n in ("mean", "cen", "sq", "var", "lnv", "rstd", "nrm", "rsq", "res", "out"):
                s[f"ln{k}_{n}"] = sem(f"ln{k}_{n}")

        def need(eng, name, count):
            if not isinstance(count, int) or count > 0:
                eng.wait_ge(s[name], count)

        def upto(pairs):
            return min(pairs, NP) if isinstance(pairs, int) else pairs

        consts = [(colt[:, :], cols), (tokw_s[:, :, :], tokw), (inw_s[:, :, :], inw), (xw_s[:, :, :], xw),
                  (dtw_s[:, :, :], dtw), (outw_s[:, :, :], outw), (qkw_s[:, :, :], qkw), (vw_s[:, :], vw),
                  (ow_s[:, :, :], ow), (w1_s[:, :, :], w1), (w2_s[:, :, :], w2), (wg_s[:, :], wg),
                  (bg_s[:, :, :], bgrow), (ident_s[:, :], ident), (spread_s[:, :], spread)]
        ALL_CONSTS = 16 * len(consts)
        PRESETS = 12

        flat = "p a b -> p (a b)"

        def iteration(steps, i, parity):
            for name in ORDER:
                lag = LAG[name[0]]
                if name not in steps or (isinstance(i, int) and not 0 <= i - lag < NP):
                    continue
                steps[name](i - lag, (parity - lag) % 2)

        def program(steps, eng):
            for i in range(-1, 4):
                iteration(steps, i, i % 2)
            with eng.Fori(2, 15) as two:
                iteration(steps, two * 2, 0)
                iteration(steps, two * 2 + 1, 1)
            for i in range(30, NP + 3):
                iteration(steps, i, i % 2)

        block = ctx.enter_context(nc.Block())

        @block.sync
        def _(sp):
            for dst, src in consts:
                sp.dma_start(dst, src).then_inc(s["consts_in"], 16)
            sp.dma_start(x_t[:, :, :], xh[0]).then_inc(s["x_in"], 16)
            sp.dma_start(h_new[:, :, NIMG:T], txt[0]).then_inc(s["txt_in"], 16)

            def waits(*counts):
                for name, count in counts:
                    sp.wait_ge(s["consts_in"], 16)
                    need(sp, name, count)

            def x_next(t, _):
                if isinstance(t, int) and t + 1 >= NP:
                    return
                waits(("tok_mm", t + 1))
                sp.dma_start(x_t[:, :, :], xh[t + 1]).then_inc(s["x_in"], 16)

            def h_store(f, _):
                waits(("tok_done", f + 1), ("txt_in", 16 * f + 16), ("h_out", 16 * f))
                sp.dma_start(h_dram[f], h_new[:, :, :]).then_inc(s["h_out"], 16)

            def txt_load(t, _):
                if isinstance(t, int) and t == 0:
                    return
                waits(("ln0_cen", t), ("h_out", 16 * t))
                sp.dma_start(h_new[:, :, NIMG:T], txt[t]).then_inc(s["txt_in"], 16)

            def bc_store(f, par):
                waits(("xd_evac", 2 * f + 2), ("drv_done", NCH * (f - 1)))
                sp.dma_start(bc_dram[par], xd[32:64, :]).then_inc(s["bc_out"], 16)

            def bc_load(g):
                def f(m, par):
                    used = NCH * m + H2 * (g - 1)
                    waits(*([("bc_out", 16 * m + 16)] if g == 0 else []), ("hc_done", used), ("drv_done", used))
                    for k in range(2):
                        rows = bc_dram[par, k * NS + NG * g:k * NS + NG * g + NG, :]
                        sp.dma_start(bc_rep[:, g % 2, k, :, :], rows.unsqueeze(0).to_broadcast([128, NG, W])
                                     ).then_inc(s[f"{'bc'[k]}_in{g % 2}"], 16)
                return f

            def h_load(e, _):
                waits(("hh_done", e), ("h_out", 16 * e + 16))
                sp.dma_start(h_res[:, :, :], h_dram[e]).then_inc(s["hres_in"], 16)

            def store(e, _):
                waits(("outb_done", e + 1))
                sp.dma_start(out[e], outb[:, :, :]).then_inc(s["out_stored"], 16)

            program({"K x": x_next, "K txt": txt_load, "F hstore": h_store, "F bcst": bc_store,
                     "F bc 0": bc_load(0), "F bc 1": bc_load(1), "C bc 2": bc_load(2), "C bc 3": bc_load(3),
                     "E hres": h_load, "E store": store}, sp)
            sp.wait_ge(s["out_stored"], 16 * NP)

        @block.gpsimd
        def _(pool):
            def drive(c):
                half, g, slot = c % H2, c // H2, c % 2

                def f(m, par):
                    n = NCH * m + c
                    if half == 0:
                        pool.wait_ge(s[f"b_in{g % 2}"], 16 * (CH // 2 * m + g // 2 + 1))
                    if c == 0:
                        pool.wait_ge(s["dtu_done"], m + 1)
                    need(pool, "scan_done", n - 1)
                    pool.tensor_tensor(drv[:, slot, :, :], dtu[:, par, half:half + 1, :].to_broadcast([128, NG, W]),
                                       bc_rep[:, g % 2, 0, :, :], ALU.mult).then_inc(s["drv_done"], 1)
                return f

            def fold(c):
                slot = c % 2

                def f(m, _):
                    n = NCH * m + c
                    pool.wait_ge(s["hc_done"], n + 1)
                    x = hst[:, slot, :, :]
                    pool.tensor_tensor(x[:, 0:2], x[:, 0:2], x[:, 2:4], ALU.add).then_inc(s["hsum_done"], 1)
                    pool.wait_ge(s["hsum_done"], n + 1)
                    pool.tensor_tensor(x[:, 0], x[:, 0], x[:, 1], ALU.add).then_inc(s["hsum2_done"], 1)
                return f

            def o_first(a, _):
                pool.wait_ge(s["rd_done"], PAIR * a + 1)
                pool.tensor_tensor(oT[:, :, 0, :], o_sb[:, :, :], rden[:, :, :], ALU.mult).then_inc(s["o0_done"], 1)

            def final(e, _):
                pool.wait_ge(s["outb_part"], PAIR * e + PAIR)
                o = outb[:, :, :].rearrange(flat)
                pool.tensor_tensor(o, o, hh[:, :], ALU.add).then_inc(s["outb_done"], 1)

            def select(e, _):
                pool.wait_ge(s["idx_done"], PAIR * e + PAIR)
                need(pool, "outb_part", PAIR * e)
                pool.tensor_tensor(top_seen[:, :, :], top8[:, :, :],
                                   ones_s[:, 0:PAIR * 8].rearrange("p (b e) -> p b e", b=PAIR), ALU.mult
                                   ).then_inc(s["top_read"], 1)
                for b in range(PAIR):
                    x = pool.value_load(idx8[0:1, b, 0:1], min_val=0, max_val=E - 1)
                    pool.dma_start(wsel[:, b, :], wexp[bass.ds(x, 1)].rearrange("a p n -> (a p) n")
                                   ).then_inc(s["wsel_in"], 16)

            pool.wait_ge(s["consts_in"], ALL_CONSTS)
            pool.wait_ge(s["preset_done"], PRESETS)
            program({f"C drv {c}": drive(c) for c in range(NCH)} | {f"C fold {c}": fold(c) for c in range(NCH)}
                    | {"A o0": o_first, "E wsel": select, "E out": final}, pool)

        @block.scalar
        def _(act):
            A = act.activation
            LOGEXP, GELU = "natural_log_exp_and_others", "gelu_and_others"
            act.wait_ge(s["consts_in"], ALL_CONSTS)
            act.wait_ge(s["preset_done"], PRESETS)
            act.preload_act_table_set(LOGEXP)
            A(a_neg[:, :], col("a_log", 0, H2 * NS), ACT.Exp).then_inc(s["a_exp"], 1)
            A(ln_unit[:, :], zero_s[:, :], ACT.Ln, bias=unit_s[:, :]).then_inc(s["a_exp"], 1)
            act.wait_ge(s["a_done"], 1)
            act.wait_ge(s["scaled_done"], 5)

            def square(k, sq_t, cen_t, ready="cen"):
                def f(r, _):
                    act.wait_ge(s[f"ln{k}_{ready}"], r + 1)
                    A(sq_t[:, :], cen_t, ACT.Square).then_inc(s[f"ln{k}_sq"], 1)
                return f

            def invert(k, rstd_t, var_ps, rsq=None, used=None):
                def f(r, par):
                    act.wait_ge(s[f"ln{k}_var"], r + 1)
                    A(rstd_t[:, :], var_ps, ACT.Ln, bias=eps_s[:, :]).then_inc(s[f"ln{k}_lnv"], 1)
                    act.wait_ge(s[f"ln{k}_lnv"], r + 1)
                    A(rstd_t[:, :], rstd_t[:, :], ACT.Exp, scale=-0.5).then_inc(s[f"ln{k}_rstd"], 1)
                    if rsq:
                        act.wait_ge(s[f"ln{k}_rstd"], r + 1)
                        need(act, used[0], used[1](r))
                        A(rsq(par), rstd_t[:, :], ACT.Square).then_inc(s[f"ln{k}_rsq"], 1)
                return f

            def u_evac(f, _):
                act.wait_ge(s["in_mm"], 2 * f + 1)
                need(act, "conv_step", H2 * (TAPS - 1) * f)
                A(u_pad[:, :, TAPS - 1:], fe[:, :, 0:W].rearrange("p h (b t) -> p h b t", b=PAIR),
                  ACT.Copy).then_inc(s["u_evac"], 1)

            def conv_first(f, _):
                act.wait_ge(s["u_evac"], f + 1)
                need(act, "dt_done", f)
                for h in range(H2):
                    A(cv[:, h, :].rearrange("p (b t) -> p b t", b=PAIR), u_pad[:, PAIR * h:PAIR * h + PAIR, 0:T],
                      ACT.Identity, bias=col("conv_b", h), scale=col("conv_w", h * TAPS)
                      ).then_inc(s["tap_done"], 1)

            def z_tanh(f, _):
                act.wait_ge(s["in_mm"], 2 * f + 2)
                need(act, "dt_done", f)
                A(zt[:, :, :], fe[:, :, 0:W], ACT.Tanh, scale=0.5).then_inc(s["zt_done"], 1)

            def u_tanh(f, _):
                act.wait_ge(s["conv_step"], H2 * (TAPS - 1) * (f + 1))
                A(th[:, :, :], cv[:, :, :], ACT.Tanh).then_inc(s["th_done"], 1)

            def xd_evac(f, _):
                act.wait_ge(s["xp_mm"], f + 1)
                need(act, "dt_mm", f)
                need(act, "bc_out", 16 * f)
                A(xd[0:RANK, :], fe[0:RANK, 1, 0:W], ACT.Copy).then_inc(s["xd_evac"], 1)
                A(xd[32:64, :], fe[32:64, 1, 0:W], ACT.Copy).then_inc(s["xd_evac"], 1)

            def sp_split(f, par):
                v = fe[:, :, 0:W]
                act.wait_ge(s["dt_mm"], f + 1)
                act.wait_ge(s["zs_done"], f + 1)
                A(sp_e[:, :, :], v, ACT.Abs).then_inc(s["sp_step"], 1)
                A(dt[:, par, :, :], v, ACT.Relu).then_inc(s["sp_step"], 1)

            def sp_exp(f, _):
                act.wait_ge(s["sp_step"], 5 * f + 1)
                A(sp_e[:, :, :], sp_e[:, :, :], ACT.Exp, scale=-1.0).then_inc(s["sp_step"], 1)

            def sp_log(f, _):
                act.wait_ge(s["sp_step"], 5 * f + 3)
                act.wait_ge(s["u_done"], f + 1)
                A(sp_l[:, :, :], sp_e[:, :, :], ACT.Relu, bias=neg_small[:, :]).then_inc(s["sp_step"], 1)
                act.wait_ge(s["sp_step"], 5 * f + 4)
                A(sp_l[:, :, :], sp_l[:, :, :], ACT.Ln, bias=unit_s[:, :],
                  scale=1 / (1 + SMALL)).then_inc(s["sp_step"], 1)

            def decay(c):
                half, g, slot = c % H2, c // H2, c % 2

                def f(m, par):
                    if c == 0:
                        act.wait_ge(s["dt_done"], m + 1)
                    need(act, "scan_done", NCH * m + c - 1)
                    src = dt[:, par, half, :].rearrange("p (b t) -> p b t", b=PAIR)[:, :, 1:T]
                    for j in range(NG):
                        k = half * NS + g * NG + j
                        last = A(dec[:, slot, j, :, 1:T], src, ACT.Exp, scale=a_neg[:, k:k + 1])
                    last.then_inc(s["dec_done"], 1)
                return f

            def qk_evac(a, _):
                act.wait_ge(s["qk_mm"], a + 1)
                for g in range(GRP):
                    A(qT[:, g, :], ap[:, g, 0:W], ACT.Identity, bias=col("bq", g),
                      scale=HD ** -0.5).then_inc(s["qk_done"], 1)
                for g in range(GRP):
                    A(kT[:, g, :], ap[:, 2 + g, 0:W], ACT.Identity, bias=col("bk", g)).then_inc(s["qk_done"], 1)

            def v_evac(a, _):
                act.wait_ge(s["v_mm"], a + 1)
                for t, (_, n) in enumerate(KTILES):
                    last = A(v_s[0:n, :, t, :, 0:HD],
                             ap[0:n, 0, 0:512].rearrange("p (b t h e) -> p b t h e", b=PAIR, t=2, h=HEADS)[:, :, t],
                             ACT.Copy)
                last.then_inc(s["v_done"], 1)

            def probs(b, t):
                n = KTILES[t][1]

                def f(a, _):
                    need(act, "pv_mm", PAIR * a + b)
                    act.wait_ge(s["st_mm"], 4 * a + 2 * b + t + 1)
                    A(pT[0:n, t, :, :].rearrange("p (g e) q -> p g (e q)", g=4), ap[0:n, :, 0:W],
                      ACT.Exp).then_inc(s["p_done"], 1)
                return f

            def o_evac(b):
                def f(a, _):
                    act.wait_ge(s["pv_mm"], PAIR * a + b + 1)
                    need(act, "o0_done" if b else "o1_done", a + b)
                    A(o_sb[:, :, :].rearrange(flat), ap[:, 0, 0:W], ACT.Copy).then_inc(s["oev_done"], 1)
                return f

            def inv_sum(b):
                def f(a, _):
                    act.wait_ge(s["sel_mm"], PAIR * a + b + 1)
                    r = rden[:, :, :].rearrange(flat)
                    A(r, ap[:, 1, 0:W], ACT.Ln).then_inc(s["rd_ln"], 1)
                    act.wait_ge(s["rd_ln"], PAIR * a + b + 1)
                    A(r, r, ACT.Exp, scale=-1.0).then_inc(s["rd_done"], 1)
                return f

            def gelu(first):
                def f(e, _):
                    need(act, "f2_mm", e)
                    for j in (first, first + 1):
                        act.wait_ge(s["f1_mm"], FC * e + j + 1)
                        A(hid[:, j, :], fe[:, j % 2, 0:W], ACT.Gelu, bias=col("b1", j)).then_inc(s["gelu_done"], 1)
                return f

            def expert(e, _):
                act.wait_ge(s["lgm_done"], PAIR * e + PAIR)
                A(lge[:, :, :], lgm[:, :, :], ACT.Exp).then_inc(s["lge_done"], 1)

            def gated_out(e, _):
                act.wait_ge(s["y2_mm"], e + 1)
                act.wait_ge(s["gbias_done"], e + 1)
                need(act, "out_stored", 16 * e)
                for b in range(PAIR):
                    A(outb[:, b, :], fe[:, 0, b * T:b * T + T], ACT.Identity, bias=gated_b[:, b:b + 1],
                      scale=gate_b[:, b:b + 1]).then_inc(s["outb_part"], 1)

            def tables(steps):
                own = [n for n in ORDER if n in ("F zt", "F th", "E ga", "E gb")]
                def loads(n):
                    step, mine = steps[n], [k for k in own if k[0] == n[0]]

                    def f(r, par):
                        i = r + LAG[n[0]]
                        alone = isinstance(i, int) and not LAG["E"] <= i < NP
                        here = mine if alone else own
                        if n == here[0]:
                            act.preload_act_table_set(GELU)
                        step(r, par)
                        if n == here[-1]:
                            act.preload_act_table_set(LOGEXP)
                    return f
                return steps | {n: loads(n) for n in own}

            program(tables(
                {"F sq": square(0, sq0, cen0[:, :]),
                 "F rstd": invert(0, rstd0, fe[:, 0, 0:W], lambda par: x0[:, par, :], ("r1_done", lambda f: f - 1)),
                 "F u_ev": u_evac, "F tap": conv_first,
                 "F zt": z_tanh, "F th": u_tanh, "F xd": xd_evac, "F sp_v": sp_split, "F sp_e": sp_exp,
                 "F sp_l": sp_log,
                 "A sq": square(1, sq1, ap[:, 3, 0:W], "mean"),
                 "A rstd": invert(1, rstd1, ap[:, 2, 0:W], lambda par: h1[:, par, :], ("r2_done", lambda a: a - 1)),
                 "A qk_ev": qk_evac,
                 "A v_ev": v_evac,
                 "E2 sq": square(2, sq, cen[:, :]), "E2 rstd": invert(2, rstd, fe[:, 1, 0:W]), "E ga": gelu(0),
                 "E gb": gelu(2),
                 "E3 sq": square(3, sq, cen[:, :]), "E3 rstd": invert(3, rstd, fe[:, 0, 0:W]),
                 "E4 sq": square(4, sq, cen[:, :]), "E4 rstd": invert(4, rstd, fe[:, 0, 0:W]), "E lge": expert,
                 "E outa": gated_out}
                | {f"C dec {c}": decay(c) for c in range(NCH)}
                | {f"A pr{b}{t}": probs(b, t) for b in range(PAIR) for t in range(2)}
                | {f"{A_OR_B[b]} o_ev{b}": o_evac(b) for b in range(PAIR)}
                | {f"{A_OR_B[b]} rd{b}": inv_sum(b) for b in range(PAIR)}), act)

        @block.tensor
        def _(pe):
            def mm(out_ps, lhsT, rhs, first=True, last=True):
                return pe.matmul(out_ps, lhsT, rhs, start=first, stop=last)

            pe.wait_ge(s["consts_in"], ALL_CONSTS)
            pe.wait_ge(s["preset_done"], PRESETS)
            pe.wait_ge(s["scaled_done"], 5)
            for g in range(GRP):
                last = mm(ap[:, 0, 0:1], ow_s[:, g, :], col("bv", g), g == 0, g == GRP - 1)
            last.then_inc(s["bvo_mm"], 1)
            pe.wait_ge(s["prep_done"], 1)

            def tok(part):
                k0, k1 = KT * part // 3, KT * (part + 1) // 3

                def f(t, _):
                    if part == 0:
                        pe.wait_ge(s["x_in"], 16 * t + 16)
                        need(pe, "sp_step", 5 * (t - 1) + 2)
                        need(pe, "gb_done", t - 3)
                    for k in range(k0, k1):
                        last = mm(fe[:, 1, 0:PAIR * NPATCH], tokw_s[:, k, :], x_t[:, k, :], k == 0, k == KT - 1)
                    if part == 2:
                        last.then_inc(s["tok_mm"], 1)
                return f

            def mean(k, bank, src, *ready, weights=mean_w):
                def f(r, _):
                    for name, count in ready:
                        need(pe, name, count(r))
                    mm(bank, weights[:, :], src).then_inc(s[f"ln{k}_mean"], 1)
                return f

            def var(k, bank, sq_t):
                def f(r, _):
                    pe.wait_ge(s[f"ln{k}_sq"], r + 1)
                    mm(bank, mean_w[:, :], sq_t[:, :]).then_inc(s[f"ln{k}_var"], 1)
                return f

            def in_u(f, par):
                pe.wait_ge(s["ln0_out"], f + 1)
                need(pe, "ln2_lnv", f - 2)
                for j in range(2):
                    last = mm(fe[:, j, 0:W], inw_s[:, j, :], x0[:, par, :])
                last.then_inc(s["in_mm"], 1)

            def in_z(f, par):
                pe.wait_ge(s["u_evac"], f + 1)
                for j in range(2):
                    last = mm(fe[:, j, 0:W], inw_s[:, 2 + j, :], x0[:, par, :])
                last.then_inc(s["in_mm"], 1)

            def x_proj(f, par):
                pe.wait_ge(s["u_done"], f + 1)
                need(pe, "gelu_done", FC * (f - 2))
                for h in range(H2):
                    last = mm(fe[0:64, 1, 0:W], xw_s[:, h, :], u[:, par, h, :], h == 0, h == H2 - 1)
                last.then_inc(s["xp_mm"], 1)

            def dt_proj(f, _):
                pe.wait_ge(s["xd_evac"], 2 * f + 2)
                need(pe, "ln3_lnv", f - 2)
                for h in range(H2):
                    last = mm(fe[:, h, 0:W], dtw_s[:, h, :], xd[0:RANK + 1, :])
                last.then_inc(s["dt_mm"], 1)

            def state_sum(c):
                half, g, slot = c % H2, c // H2, c % 2

                def f(m, _):
                    pe.wait_ge(s["hsum2_done"], NCH * m + c + 1)
                    if c == 0:
                        need(pe, "r1_done", m)
                    mm(yp[:, half, 0:W], ident_s[:, :], hst[:, slot, 0, :], g == 0, g == CH - 1
                       ).then_inc(s["y_mm"], 1)
                return f

            def out_proj(m, _):
                pe.wait_ge(s["g_done"], m + 1)
                for h in range(H2):
                    last = mm(yp[:, 0, 0:W], outw_s[:, h, :], ypd[:, h, :], h == 0, h == H2 - 1)
                last.then_inc(s["op_mm"], 1)

            def qk(a, par):
                pe.wait_ge(s["ln1_out"], a + 1)
                need(pe, "r2_done", a)
                for g in range(2 * GRP):
                    last = mm(ap[:, g, 0:W], qkw_s[:, g, :], h1[:, par, :])
                last.then_inc(s["qk_mm"], 1)

            def values(a, par):
                pe.wait_ge(s["qk_done"], 4 * a + 1)
                for b in range(PAIR):
                    for t, (k0, n) in enumerate(KTILES):
                        o = (2 * b + t) * D
                        last = mm(ap[0:n, 0, o:o + D], h1[:, par, b * T + k0:b * T + k0 + n], vw_s[:, :])
                last.then_inc(s["v_mm"], 1)

            def scores(b, t):
                k0, n = KTILES[t]

                def f(a, _):
                    if t:
                        pe.wait_ge(s["max_done"], 4 * a + 2 * b + 1)
                    elif b:
                        pe.wait_ge(s["rd_ln"], PAIR * a + 1)
                    else:
                        pe.wait_ge(s["qk_done"], 4 * a + 4)
                        pe.wait_ge(s["v_done"], a + 1)
                    for e in range(GRP):
                        for g in range(4):
                            rows = slice(QUAD * g, QUAD * g + QUAD)
                            last = mm(ap[0:n, g, e * T:e * T + T], qT[rows, e, b * T + k0:b * T + k0 + n],
                                      kT[rows, e, b * T:b * T + T])
                    last.then_inc(s["s_mm"], 1)
                return f

            def turn(b):
                def f(a, _):
                    pe.wait_ge(s["max_done"], 4 * a + 2 * b + 2)
                    for e in range(GRP):
                        for t, (k0, n) in enumerate(KTILES):
                            last = pe.transpose(ap[:, 0, e * T + k0:e * T + k0 + n],
                                                negm[0:n, t, e, :, :].rearrange(flat), ident_s[0:n, 0:n])
                    last.then_inc(s["mt_mm"], 1)
                return f

            def scores_t(b, t):
                k0, n = KTILES[t]

                def f(a, _):
                    if t:
                        pe.wait_ge(s["p_done"], 4 * a + 2 * b + 1)
                    else:
                        pe.wait_ge(s["qaug_done"], PAIR * a + b + 1)
                    for e in range(GRP):
                        for g in range(4):
                            rows = slice(QUAD * g, QUAD * g + QUAD)
                            last = mm(ap[0:n, g, e * T:e * T + T], kT[rows, e, b * T + k0:b * T + k0 + n],
                                      qT[rows, e, b * T:b * T + T])
                    last.then_inc(s["st_mm"], 1)
                return f

            def pv(b):
                def f(a, _):
                    pe.wait_ge(s["p_done"], 4 * a + 2 * b + 2)
                    for e in range(GRP):
                        for t, (_, n) in enumerate(KTILES):
                            for g in range(4):
                                last = mm(ap[QUAD * g:QUAD * g + QUAD, 0, e * T:e * T + T],
                                          v_s[0:n, b, t, 4 * e + g, :], pT[0:n, t, GRP * g + e, :], t == 0, t == 1)
                    last.then_inc(s["pv_mm"], 1)
                return f

            def sums_to_rows(b):
                def f(a, _):
                    pe.wait_ge(s["oev_done"], PAIR * a + b + 1)
                    mm(ap[:, 1, 0:W], spread_s[:, :], o_sb[:, :, :].rearrange(flat)).then_inc(s["sel_mm"], 1)
                return f

            def attn_out(a, _):
                pe.wait_ge(s["o0_done"], a + 1)
                pe.wait_ge(s["o1_done"], a + 1)
                for g in range(GRP):
                    last = mm(ap[:, 0, 0:W], ow_s[:, g, :], oT[:, g, :, :].rearrange(flat), g == 0, g == GRP - 1)
                last.then_inc(s["ao_mm"], 1)

            def ffn1(first):
                def f(e, _):
                    if first:
                        pe.wait_ge(s["gelu_done"], FC * e + 2)
                    else:
                        pe.wait_ge(s["ln2_out"], e + 1)
                        need(pe, "zs_done", upto(e + 4))
                    for j in (first, first + 1):
                        mm(fe[:, j % 2, 0:W], w1_s[:, j, :], h2[:, :]).then_inc(s["f1_mm"], 1)
                return f

            def ffn2(e, _):
                pe.wait_ge(s["gelu_done"], FC * e + FC)
                for j in range(FC):
                    last = mm(fe[:, 0, 0:W], w2_s[:, j, :], hid[:, j, :], j == 0, j == FC - 1)
                last.then_inc(s["f2_mm"], 1)

            def logits(e, _):
                pe.wait_ge(s["msum_done"], e + 1)
                for b in range(PAIR):
                    last = mm(fe[0:1, 0, b * E:b * E + E], msum[:, b:b + 1], wg_s[:, :])
                last.then_inc(s["lg_mm"], 1)

            def gates(e, _):
                pe.wait_ge(s["gate_done"], e + 1)
                need(pe, "sp_step", 5 * (upto(e + 4) - 1) + 2)
                mm(fe[:, 1, 0:PAIR], ones_s[:, :], gate[:, :]).then_inc(s["gb_mm"], 1)

            def expert(e, _):
                pe.wait_ge(s["wsel_in"], 16 * PAIR * (e + 1))
                pe.wait_ge(s["gate_done"], e + 1)
                for b in range(PAIR):
                    last = mm(fe[:, 0, b * T:b * T + T], wsel[:, b, 0:D], xm[:, b, :])
                last.then_inc(s["y2_mm"], 1)

            program(
                {"K mm0": tok(0), "K mm1": tok(1), "K mm2": tok(2),
                 "F mean": mean(0, fe[:, 0, 0:W], h_new[:, :, :].rearrange(flat), ("tok_done", lambda f: f + 1),
                                ("txt_in", lambda f: 16 * f + 16), ("outb_part", lambda f: PAIR * (f - 3))),
                 "F var": var(0, fe[:, 0, 0:W], sq0), "F in_u": in_u, "F in_z": in_z, "F xp": x_proj, "F dt": dt_proj,
                 "C out": out_proj,
                 "A mean": mean(1, ap[:, 3, 0:W], r1[:, :], ("r1_done", lambda a: a + 1), ("p_done", lambda a: 4 * a),
                                weights=center_w),
                 "A var": var(1, ap[:, 2, 0:W], sq1), "A qk": qk, "A v": values, "B ao": attn_out,
                 "E2 mean": mean(2, fe[:, 1, 0:W], r2[:, :], ("r2_done", lambda e: e + 1),
                                 ("tok_done", lambda e: upto(e + 4))),
                 "E2 var": var(2, fe[:, 1, 0:W], sq), "E f1a": ffn1(0), "E f1b": ffn1(2), "E f2": ffn2,
                 "E3 mean": mean(3, fe[:, 0, 0:W], r3[:, :], ("r3_done", lambda e: e + 1)),
                 "E3 var": var(3, fe[:, 0, 0:W], sq),
                 "E4 mean": mean(4, fe[:, 0, 0:W], hh[:, :], ("hh_done", lambda e: e + 1),
                                 ("sp_step", lambda e: 5 * (upto(e + 4) - 1) + 2)),
                 "E4 var": var(4, fe[:, 0, 0:W], sq), "E lg": logits, "E gbm": gates, "E y2": expert}
                | {f"C sum {c}": state_sum(c) for c in range(NCH)}
                | {f"A s{b}{t}": scores(b, t) for b in range(PAIR) for t in range(2)}
                | {f"A st{b}{t}": scores_t(b, t) for b in range(PAIR) for t in range(2)}
                | {f"A mt{b}": turn(b) for b in range(PAIR)} | {f"A pv{b}": pv(b) for b in range(PAIR)}
                | {f"{A_OR_B[b]} sel{b}": sums_to_rows(b) for b in range(PAIR)}, pe)

        @block.vector
        def _(dve):
            V = dve

            def stt(out_, in0, scalar, in1, op0, op1):
                return V.scalar_tensor_tensor(out=out_, in0=in0, scalar=scalar, in1=in1, op0=op0, op1=op1)

            for t_, val in ((mean_w[:, :], 1.0 / D), (ones_s[:, :], 1.0), (eps_s[:, :], EPS),
                            (zero_s[:, :], 0.0), (neg_small[:, :], -SMALL), (unit_s[:, :], 1.0),
                            (u_pad[:, :, 0:TAPS - 1], 0.0), (dec[:, :, :, :, 0:1], 0.0), (xd[0:32, :], 1.0),
                            (v_s[:, :, :, :, HD:QUAD], 1.0), (negm[:, :, :, :, :], 0.0)):
                V.memset(t_, val).then_inc(s["preset_done"], 1)
            V.wait_ge(s["consts_in"], ALL_CONSTS)
            for b in range(PAIR):
                last = V.tensor_tensor(h_new[:, b, 0:1], col("cls"), col("pos"), ALU.mult)
            last.then_inc(s["preset_done"], 1)
            c0 = COLS["conv_w"][0]
            cw = colt[:, c0:c0 + H2 * TAPS + H2]
            V.tensor_scalar(cw, cw, 0.5, None, ALU.mult).then_inc(s["scaled_done"], 1)
            V.tensor_scalar(outw_s[:, :, :], outw_s[:, :, :], 0.5, None, ALU.mult).then_inc(s["scaled_done"], 1)
            bq = col("bq", 0, GRP)
            V.tensor_scalar(bq, bq, HD ** -0.5, None, ALU.mult).then_inc(s["scaled_done"], 1)
            V.tensor_scalar(col("g1"), col("g1"), -0.5, None, ALU.mult).then_inc(s["scaled_done"], 1)
            V.wait_ge(s["preset_done"], 1)
            V.tensor_tensor(center_w[:, :], ident_s[:, :], mean_w[:, :], ALU.subtract).then_inc(s["scaled_done"], 1)
            V.wait_ge(s["a_exp"], 2)
            V.tensor_scalar(a_neg[:, :], a_neg[:, :], -1.0, None, ALU.mult).then_inc(s["a_done"], 1)
            V.wait_ge(s["bvo_mm"], 1)
            V.tensor_tensor(bo_all[:, :], ap[:, 0, 0:1], col("bo"), ALU.add).then_inc(s["prep_done"], 1)
            V.wait_ge(s["scaled_done"], 5)
            V.wait_ge(s["preset_done"], PRESETS)
            V.wait_ge(s["prep_done"], 1)

            def pos(t, _):
                V.wait_ge(s["tok_mm"], t + 1)
                need(V, "h_out", 16 * t)
                p = col("pos", 1, NPATCH).unsqueeze(1).to_broadcast([128, PAIR, NPATCH])
                stt(h_new[:, :, 1:NIMG], fe[:, 1, 0:PAIR * NPATCH].rearrange("p (b n) -> p b n", b=PAIR),
                    col("tok_b"), p, ALU.add, ALU.mult).then_inc(s["tok_done"], 1)

            def center(k, src, mean_ps, cen_t):
                def f(r, _):
                    V.wait_ge(s[f"ln{k}_mean"], r + 1)
                    V.tensor_tensor(cen_t[:, :], src, mean_ps, ALU.subtract).then_inc(s[f"ln{k}_cen"], 1)
                return f

            def scale(k, cen_t, rstd_t, dst):
                def f(r, _):
                    V.wait_ge(s[f"ln{k}_rstd"], r + 1)
                    stt(cen_t[:, :], cen_t[:, :], col(f"g{k}"), rstd_t[:, :], ALU.mult, ALU.mult
                        ).then_inc(s[f"ln{k}_nrm"], 1)
                    V.wait_ge(s[f"ln{k}_nrm"], r + 1)
                    V.tensor_scalar(dst, cen_t[:, :], col(f"e{k}"), None, ALU.add).then_inc(s[f"ln{k}_out"], 1)
                return f

            def newton(k, r, rsq, var_ps, nrm, dst):
                V.wait_ge(s[f"ln{k}_rsq"], r + 1)
                stt(rsq, var_ps, eps_s[:, :], rsq, ALU.add, ALU.mult).then_inc(s[f"ln{k}_res"], 1)
                V.wait_ge(s[f"ln{k}_nrm"], r + 1)
                V.wait_ge(s[f"ln{k}_res"], r + 1)
                return stt(dst, rsq, 3.0, nrm, ALU.subtract, ALU.mult)

            def x0_out(f, par):
                V.wait_ge(s["ln0_rstd"], f + 1)
                stt(cen0[:, :], cen0[:, :], -0.5, rstd0[:, :], ALU.mult, ALU.mult).then_inc(s["ln0_nrm"], 1)
                newton(0, f, x0[:, par, :], fe[:, 0, 0:W], cen0[:, :], x0[:, par, :]).then_inc(s["ln0_out"], 1)

            def conv(k):
                def f(r, _):
                    for h in range(H2):
                        dst = cv[:, h, :].rearrange("p (b t) -> p b t", b=PAIR)
                        if k == 1:
                            V.wait_ge(s["tap_done"], H2 * r + h + 1)
                        else:
                            V.wait_ge(s["conv_step"], H2 * (TAPS - 1) * r + H2 * (k - 2) + h + 1)
                        stt(dst, u_pad[:, PAIR * h:PAIR * h + PAIR, k:k + T], col("conv_w", h * TAPS + k), dst,
                            ALU.mult, ALU.add).then_inc(s["conv_step"], 1)
                return f

            def z_silu(f, par):
                V.wait_ge(s["zt_done"], f + 1)
                stt(zs[:, par, :, :], zt[:, :, :], 1.0, fe[:, :, 0:W], ALU.add, ALU.mult).then_inc(s["zs_done"], 1)

            def u_silu(f, par):
                V.wait_ge(s["th_done"], f + 1)
                stt(u[:, par, :, :], th[:, :, :], 1.0, cv[:, :, :], ALU.add, ALU.mult).then_inc(s["u_done"], 1)

            def series0(f, par):
                c, p = sp_c[:, :, :], dtu[:, par, :, :]
                V.wait_ge(s["sp_step"], 5 * f + 3)
                need(V, "drv_done", NCH * (f - 1))
                V.tensor_scalar(c, sp_e[:, :, :], SMALL, None, ALU.min).then_inc(s["lp_step"], 1)
                V.wait_ge(s["lp_step"], 5 * f + 1)
                V.tensor_scalar(p, c, LN_3, LN_2, ALU.mult, ALU.add).then_inc(s["lp_step"], 1)

            def series1(f, par):
                p = dtu[:, par, :, :]
                V.wait_ge(s["lp_step"], 5 * f + 2)
                V.tensor_tensor(p, p, sp_c[:, :, :], ALU.mult).then_inc(s["lp_step"], 1)

            def series2(f, par):
                p = dtu[:, par, :, :]
                V.wait_ge(s["lp_step"], 5 * f + 3)
                stt(p, p, 1.0, sp_c[:, :, :], ALU.add, ALU.mult).then_inc(s["lp_step"], 1)

            def dt_log(f, par):
                p = dtu[:, par, :, :]
                V.wait_ge(s["lp_step"], 5 * f + 4)
                V.wait_ge(s["sp_step"], 5 * f + 5)
                stt(p, sp_l[:, :, :], ln_unit[:, :], p, ALU.subtract, ALU.add).then_inc(s["lp_step"], 1)

            def dt_sum(f, par):
                d = dt[:, par, :, :]
                V.wait_ge(s["lp_step"], 5 * f + 5)
                V.tensor_tensor(d, d, dtu[:, par, :, :], ALU.add).then_inc(s["dt_done"], 1)

            def dt_u(f, par):
                V.wait_ge(s["dt_done"], f + 1)
                V.tensor_tensor(dtu[:, par, :, :], dt[:, par, :, :], u[:, par, :, :], ALU.mult
                                ).then_inc(s["dtu_done"], 1)

            def scan(c):
                slot = c % 2

                def f(m, _):
                    n = NCH * m + c
                    V.wait_ge(s["dec_done"], n + 1)
                    V.wait_ge(s["drv_done"], n + 1)
                    need(V, "y_mm", n - 1)
                    V.tensor_tensor_scan(hst[:, slot, :, :].rearrange(flat),
                                         dec[:, slot, :, :, :].rearrange("p j b t -> p (j b t)"),
                                         drv[:, slot, :, :].rearrange(flat), 0.0, ALU.mult,
                                         ALU.add).then_inc(s["scan_done"], 1)
                return f

            def times_c(c):
                g, slot = c // H2, c % 2

                def f(m, _):
                    V.wait_ge(s["scan_done"], NCH * m + c + 1)
                    if c % H2 == 0:
                        V.wait_ge(s[f"c_in{g % 2}"], 16 * (CH // 2 * m + g // 2 + 1))
                    x = hst[:, slot, :, :]
                    V.tensor_tensor(x, x, bc_rep[:, g % 2, 1, :, :], ALU.mult).then_inc(s["hc_done"], 1)
                return f

            def skip(h):
                def f(m, par):
                    V.wait_ge(s["y_mm"], NCH * m + NCH - 1 + h)
                    stt(ypd[:, h, :], u[:, par, h, :], col("dp", h), yp[:, h, 0:W], ALU.mult,
                        ALU.add).then_inc(s["ypd_done"], 1)
                return f

            def gated(m, par):
                V.wait_ge(s["ypd_done"], H2 * m + H2)
                V.tensor_tensor(ypd[:, :, :], ypd[:, :, :], zs[:, par, :, :], ALU.mult).then_inc(s["g_done"], 1)

            def r1_out(m, par):
                V.wait_ge(s["op_mm"], m + 1)
                need(V, "ln1_mean", m)
                V.tensor_tensor(r1[:, :], yp[:, 0, 0:W], x0[:, par, :], ALU.add).then_inc(s["r1_done"], 1)

            def h1_out(a, par):
                V.wait_ge(s["ln1_rstd"], a + 1)
                stt(cen1[:, :], ap[:, 3, 0:W], col("g1"), rstd1[:, :], ALU.mult, ALU.mult).then_inc(s["ln1_nrm"], 1)
                newton(1, a, h1[:, par, :], ap[:, 2, 0:W], cen1[:, :], cen1[:, :]).then_inc(s["h1_scaled"], 1)
                V.wait_ge(s["h1_scaled"], a + 1)
                V.tensor_scalar(h1[:, par, :], cen1[:, :], col("e1"), None, ALU.add).then_inc(s["ln1_out"], 1)

            def maxima(b, t):
                n = KTILES[t][1]

                def f(a, _):
                    V.wait_ge(s["s_mm"], 4 * a + 2 * b + t + 1)
                    V.tensor_reduce(negm[0:n, t, :, :, HD].rearrange("p e g -> p g e"),
                                    ap[0:n, :, 0:W].rearrange("p g (e k) -> p g e k", e=GRP),
                                    AX.X, ALU.max, negate=True).then_inc(s["max_done"], 1)
                return f

            def q_augment(b):
                def f(a, _):
                    V.wait_ge(s["mt_mm"], PAIR * a + b + 1)
                    q = qT[:, :, b * T:b * T + T]
                    V.tensor_tensor(q, q, ap[:, 0, 0:W].rearrange("p (e k) -> p e k", e=GRP),
                                    ALU.add).then_inc(s["qaug_done"], 1)
                return f

            def o_second(a, _):
                V.wait_ge(s["rd_done"], PAIR * a + PAIR)
                V.tensor_tensor(oT[:, :, 1, :], o_sb[:, :, :], rden[:, :, :], ALU.mult).then_inc(s["o1_done"], 1)

            def r2_out(a, par):
                V.wait_ge(s["ao_mm"], a + 1)
                stt(r2[:, :], ap[:, 0, 0:W], bo_all[:, :], h1[:, par, :], ALU.add, ALU.add).then_inc(s["r2_done"], 1)

            def r3_out(e, _):
                V.wait_ge(s["f2_mm"], e + 1)
                stt(r3[:, :], fe[:, 0, 0:W], col("b2"), h2[:, :], ALU.add, ALU.add).then_inc(s["r3_done"], 1)

            def scale3(e, _):
                V.wait_ge(s["ln3_rstd"], e + 1)
                stt(cen[:, :], cen[:, :], col("g3"), rstd[:, :], ALU.mult, ALU.mult).then_inc(s["ln3_nrm"], 1)

            def add_res(e, _):
                V.wait_ge(s["ln3_nrm"], e + 1)
                V.wait_ge(s["hres_in"], 16 * e + 16)
                need(V, "outb_done", e)
                stt(hh[:, :], cen[:, :], col("e3"), h_res[:, :, :].rearrange(flat), ALU.add, ALU.add
                    ).then_inc(s["hh_done"], 1)

            def xm_out(e, _):
                V.wait_ge(s["ln4_rstd"], e + 1)
                V.tensor_tensor(xm[:, :, :].rearrange(flat), cen[:, :], rstd[:, :], ALU.mult).then_inc(s["ln4_out"], 1)

            def pool_tokens(e, _):
                V.wait_ge(s["ln4_out"], e + 1)
                V.tensor_reduce(msum[:, :], xm[:, :, :], AX.X, ALU.add).then_inc(s["msum_done"], 1)

            def top(e, _):
                V.wait_ge(s["lg_mm"], e + 1)
                stt(lg[:, :, :], fe[0:1, 0, 0:PAIR * E].rearrange("p (b e) -> p b e", b=PAIR), 1.0 / T, bg_s[:, :, :],
                    ALU.mult, ALU.add).then_inc(s["lg_done"], 1)
                V.wait_ge(s["lg_done"], e + 1)
                need(V, "wsel_in", 16 * PAIR * e)
                need(V, "top_read", e)
                V.tensor_copy(lg_seen[:, :, :], lg[:, :, :])
                for b in range(PAIR):
                    V.max(top8[:, b, :], lg[:, b, :]).then_inc(s["top_done"], 1)
                for b in range(PAIR):
                    V.wait_ge(s["top_done"], PAIR * e + b + 1)
                    V.tensor_scalar(lgm[:, b, :], lg[:, b, :], top8[:, b, 0:1], None,
                                    ALU.subtract).then_inc(s["lgm_done"], 1)
                    V.max_index(idx8[:, b, :], top8[:, b, :], lg[:, b, :]).then_inc(s["idx_done"], 1)

            def gate_out(e, _):
                V.wait_ge(s["lge_done"], e + 1)
                V.tensor_reduce(den2[:, :], lge[:, :, :], AX.X, ALU.add).then_inc(s["den_done"], 1)
                V.wait_ge(s["den_done"], e + 1)
                V.reciprocal(gate[:, :], den2[:, :]).then_inc(s["gate_done"], 1)

            def gate_copy(e, _):
                V.wait_ge(s["gb_mm"], e + 1)
                V.tensor_copy(gate_b[:, :], fe[:, 1, 0:PAIR]).then_inc(s["gb_done"], 1)

            def gate_bias(e, _):
                V.wait_ge(s["gb_done"], e + 1)
                V.wait_ge(s["wsel_in"], 16 * PAIR * (e + 1))
                V.tensor_tensor(gated_b[:, :], gate_b[:, :], wsel[:, :, D], ALU.mult).then_inc(s["gbias_done"], 1)

            program(
                {"K pos": pos,
                 "F cen": center(0, h_new[:, :, :].rearrange(flat), fe[:, 0, 0:W], cen0), "F x0": x0_out,
                 **{f"F cv{k}": conv(k) for k in range(1, TAPS)}, "F zs": z_silu, "F u": u_silu,
                 "F poly0": series0, "F poly1": series1,
                 "F poly2": series2, "F dtl": dt_log, "F dts": dt_sum, "F dtu": dt_u,
                 "C y0": skip(0), "C y1": skip(1), "C g": gated, "C r1": r1_out,
                 "A nrm": h1_out,
                 "B r2": r2_out,
                 "E2 cen": center(2, r2[:, :], fe[:, 1, 0:W], cen), "E2 nrm": scale(2, cen, rstd, h2[:, :]),
                 "E r3": r3_out,
                 "E3 cen": center(3, r3[:, :], fe[:, 0, 0:W], cen), "E3 nrm": scale3,
                 "E hh": add_res,
                 "E4 cen": center(4, hh[:, :], fe[:, 0, 0:W], cen), "E4 xm": xm_out, "E msum": pool_tokens,
                 "E top": top, "E gate": gate_out, "E gbc": gate_copy, "E gbias": gate_bias}
                | {f"C scan {c}": scan(c) for c in range(NCH)} | {f"C hc {c}": times_c(c) for c in range(NCH)}
                | {f"A max{b}{t}": maxima(b, t) for b in range(PAIR) for t in range(2)}
                | {f"A qaug{b}": q_augment(b) for b in range(PAIR)} | {"B o1": o_second}, dve)


def _layout(a):
    f = np.float32

    def heads(x):
        o = np.zeros((GRP, 4, QUAD) + x.shape[1:], f)
        o[:, :, :HD] = x.reshape((GRP, 4, HD) + x.shape[1:])
        return o.reshape((GRP, 4 * QUAD) + x.shape[1:])

    x = a["x"].reshape(NP, PAIR, C_IN, GRID, PATCH, GRID, PATCH).transpose(0, 2, 4, 6, 1, 3, 5)
    lay = {"xh": x.reshape(NP, KP, KT, PAIR * NPATCH)}
    lay["txt"] = a["txt"].reshape(NP, PAIR, NTXT, D).transpose(0, 3, 1, 2)
    lay["tokw"] = a["L0_tok_W"].T.reshape(KP, KT, D)
    inw = a["L0_attn_in_proj_w"].T.reshape(D, 4, 128)
    lay["inw"] = inw
    xp = a["L0_attn_x_proj_w"]
    xw = np.zeros((64, DI), f)
    xw[0:RANK], xw[32:64] = xp[0:RANK], xp[RANK:]
    lay["xw"] = xw.T.reshape(H2, 128, 64).transpose(1, 0, 2)
    dtw = np.concatenate([a["L0_attn_dt_proj_w"].T, a["L0_attn_dt_proj_b"][None]], 0)
    lay["dtw"] = dtw.reshape(RANK + 1, H2, 128)
    lay["outw"] = a["L0_attn_out_proj_w"].T.reshape(H2, 128, D).transpose(1, 0, 2)
    qw, kw, vw = a["L0_attn_mha_in_w"].reshape(3, D, D)
    qb, kb, vb = a["L0_attn_mha_in_b"].reshape(3, D)
    lay["qkw"] = np.concatenate([heads(qw), heads(kw)], 0).transpose(2, 0, 1)
    lay["vw"] = vw.T
    lay["ow"] = heads(a["L0_attn_mha_out_w"].T).transpose(1, 0, 2)
    lay["w1"] = a["L0_attn_w1"].T.reshape(D, FC, 128)
    lay["w2"] = a["L0_attn_w2"].T.reshape(FC, 128, D).transpose(1, 0, 2)
    lay["wg"] = a["L0_ffn_Wg"]
    lay["bgrow"] = np.stack([a["L0_ffn_bg"]] * PAIR)[None]
    wexp = np.concatenate([a["L0_ffn_We"].transpose(1, 0, 2), a["L0_ffn_be"].T[:, :, None]], 2)
    lay["wexp"] = wexp.transpose(1, 0, 2)
    lay["ident"] = np.eye(128, dtype=f)
    spread = np.zeros((4, QUAD, 4, QUAD), f)
    for g in range(4):
        spread[g, HD, g] = 1.0
    lay["spread"] = spread.reshape(128, 128)

    def half(v):
        return v.reshape(H2, 128, -1).transpose(1, 0, 2).reshape(128, -1)

    bk = heads(kb).reshape(GRP, 4, QUAD)
    bk[:, :, HD] = 1.0
    parts = {
        "tok_b": a["L0_tok_b"], "cls": a["L0_tok_class_token"][0], "pos": a["L0_tok_pos_embed"].T,
        "conv_w": half(a["L0_attn_conv_w"]), "conv_b": half(a["L0_attn_conv_b"]), "a_log": half(a["L0_attn_A_log"]),
        "dp": half(a["L0_attn_Dp"]), "bq": heads(qb).T, "bk": bk.reshape(GRP, 128).T, "bv": heads(vb).T,
        "bo": a["L0_attn_mha_out_b"], "g1": a["L0_attn_ln1_g"], "e1": a["L0_attn_ln1_b"], "g2": a["L0_attn_ln2_g"],
        "e2": a["L0_attn_ln2_b"], "g3": a["L0_attn_ln3_g"], "e3": a["L0_attn_ln3_b"],
        "b1": a["L0_attn_b1"].reshape(FC, 128).T, "b2": a["L0_attn_b2"]}
    lay["cols"] = np.concatenate([parts[n].reshape(128, w) for n, (_, w) in COLS.items()], 1)
    return lay


_ORDER = ["xh", "txt", "cols", "tokw", "inw", "xw", "dtw", "outw", "qkw", "vw", "ow", "w1", "w2", "wg", "bgrow",
          "wexp", "ident", "spread"]


def kernel(**inputs):
    import concourse.bacc as _bacc
    from concourse.bass_utils import run_bass_kernel_spmd as _run

    lay = _layout({k: np.asarray(v) for k, v in inputs.items()})
    nc = _bacc.Bacc("TRN2", target_bir_lowering=False, num_devices=1)
    arrays, args = {}, []
    for name in _ORDER:
        arr = np.ascontiguousarray(lay[name])
        arrays[f"in_{name}"] = arr
        args.append(nc.dram_tensor(f"in_{name}", arr.shape, mybir.dt.from_np(arr.dtype), kind="ExternalInput").ap())
    args.append(nc.dram_tensor("out_0", (NP, D, PAIR, T), F32, kind="ExternalOutput").ap())
    fusion_kernel(nc, *args)
    r = _run(nc, [arrays], core_ids=[0])
    got = r.results[0]["out_0"]
    return np.ascontiguousarray(got.transpose(0, 2, 3, 1).reshape(B, T, D))
```
